# Optimizing a Trainium2 kernel written in Bass

```python
import numpy as np
import jax
import jax.numpy as jnp

def _softmax(x, axis=-1):
    return jax.nn.softmax(x, axis=axis)

def _gelu(x):
    return jax.nn.gelu(x, approximate=True)

def _silu(x):
    return jax.nn.silu(x)

def _sigmoid(x):
    return jax.nn.sigmoid(x)

def _layernorm(x, axis=-1, eps=1e-05):
    m = jnp.mean(x, axis=axis, keepdims=True)
    v = jnp.var(x, axis=axis, keepdims=True)
    return (x - m) / jnp.sqrt(v + eps)

def _scatter_add(tgt, idx, src, axis=0):
    return tgt.at[idx].add(src)

def _segment_sum(src, seg, n):
    return jax.ops.segment_sum(src, seg, n)
kernel_name = 'mk_gnn_resnorm_d2_gnn_r8_1ce8ad'

def setup_inputs(seed: int=0):
    np.random.seed(seed)
    _w = jnp.asarray

    def _rec_inputs():
        import jax
        import jax.numpy as jnp
        _gk = jax.random.key(seed)
        x = -0.0003713 + 1 * jax.random.normal(jax.random.fold_in(_gk, 1), (6250, 128), jnp.float32)
        src = jax.random.randint(jax.random.fold_in(_gk, 2), (100000,), 0, 6250, jnp.int32)
        dst = jnp.minimum((6250 * jax.random.uniform(jax.random.fold_in(_gk, 3), (100000,)) ** 2.0).astype(jnp.int32), 49999)
        _o = jnp.argsort(dst, stable=True)
        src = src[_o]
        dst = dst[_o]
        edge_attr_64 = 0.000102155 + 1.00015 * jax.random.normal(jax.random.fold_in(_gk, 11), (100000, 64), jnp.float32)
        edge_weight = jax.random.uniform(jax.random.fold_in(_gk, 13), (100000,), jnp.float32, 0.0, 0.999999)
        return (x, src, dst, edge_attr_64, edge_weight)
    x, src, dst, edge_attr_64, edge_weight = _rec_inputs()

    def _L0_gnn_setup():
        import jax, jax.numpy as jnp
        import numpy as np
        N_NODES = 12500
        N_EDGES = 62500
        IN_CH = 128
        EDGE_CH = 64

        def _glorot(key, shape):
            fan_in, fan_out = (shape[0], shape[1])
            lim = (6.0 / (fan_in + fan_out)) ** 0.5
            return jax.random.uniform(key, shape, jnp.float32, -lim, lim)
        key = jax.random.key(seed)
        ks = jax.random.split(key, 14)
        x = jax.random.normal(ks[0], (N_NODES, IN_CH), jnp.float32)
        edge_index = jax.random.randint(ks[1], (2, N_EDGES), 0, N_NODES, jnp.int64)
        edge_attr = jax.random.normal(ks[2], (N_EDGES, EDGE_CH), jnp.float32)
        timestamps = jax.random.uniform(ks[3], (N_EDGES,), jnp.float32)
        We1 = _glorot(ks[4], (EDGE_CH, 2 * EDGE_CH))
        be1 = jnp.zeros((2 * EDGE_CH,), jnp.float32)
        We2 = _glorot(ks[5], (2 * EDGE_CH, IN_CH))
        be2 = jnp.zeros((IN_CH,), jnp.float32)
        Wt = _glorot(ks[6], (1, IN_CH))
        bt = jnp.zeros((IN_CH,), jnp.float32)
        Wn1 = _glorot(ks[7], (2 * IN_CH, IN_CH))
        bn1 = jnp.zeros((IN_CH,), jnp.float32)
        Wn2 = _glorot(ks[8], (IN_CH, IN_CH))
        bn2 = jnp.zeros((IN_CH,), jnp.float32)
        return {'x': x, 'edge_index': edge_index, 'edge_attr': edge_attr, 'timestamps': timestamps, 'We1': We1, 'be1': be1, 'We2': We2, 'be2': be2, 'Wt': Wt, 'bt': bt, 'Wn1': Wn1, 'bn1': bn1, 'Wn2': Wn2, 'bn2': bn2}
    _L0_gnn_all = _L0_gnn_setup()
    _L0_gnn_in = {k: v for k, v in _L0_gnn_all.items() if k in ('We1', 'be1', 'We2', 'be2', 'Wt', 'bt', 'Wn1', 'bn1', 'Wn2', 'bn2')}
    del _L0_gnn_all

    def _L1_gnn_setup():
        import jax, jax.numpy as jnp
        import numpy as np
        N_NODES = 6250
        N_EDGES = 62500
        D = 128
        key = jax.random.key(seed)
        ks = jax.random.split(key, 8)
        scale = 1.0 / np.sqrt(D)
        x = jax.random.normal(ks[0], (N_NODES, D), dtype=jnp.float32)
        edge_index = jax.random.randint(ks[1], (2, N_EDGES), 0, N_NODES, dtype=jnp.int64)
        return {'x': x, 'edge_index': edge_index, 'W_rel0': jax.random.normal(ks[2], (D, D), dtype=jnp.float32) * scale, 'b_rel0': jnp.zeros((D,), dtype=jnp.float32), 'W_root0': jax.random.normal(ks[3], (D, D), dtype=jnp.float32) * scale, 'W_rel1': jax.random.normal(ks[4], (D, D), dtype=jnp.float32) * scale, 'b_rel1': jnp.zeros((D,), dtype=jnp.float32), 'W_root1': jax.random.normal(ks[5], (D, D), dtype=jnp.float32) * scale}
    _L1_gnn_all = _L1_gnn_setup()
    _L1_gnn_in = {k: v for k, v in _L1_gnn_all.items() if k in ('W_rel0', 'b_rel0', 'W_root0', 'W_rel1', 'b_rel1', 'W_root1')}
    del _L1_gnn_all
    return {'x': x, 'src': src, 'dst': dst, 'edge_attr_64': edge_attr_64, 'edge_weight': edge_weight, 'L0_gnn_We1': _L0_gnn_in['We1'], 'L0_gnn_be1': _L0_gnn_in['be1'], 'L0_gnn_We2': _L0_gnn_in['We2'], 'L0_gnn_be2': _L0_gnn_in['be2'], 'L0_gnn_Wt': _L0_gnn_in['Wt'], 'L0_gnn_bt': _L0_gnn_in['bt'], 'L0_gnn_Wn1': _L0_gnn_in['Wn1'], 'L0_gnn_bn1': _L0_gnn_in['bn1'], 'L0_gnn_Wn2': _L0_gnn_in['Wn2'], 'L0_gnn_bn2': _L0_gnn_in['bn2'], 'L1_gnn_W_rel0': _L1_gnn_in['W_rel0'], 'L1_gnn_b_rel0': _L1_gnn_in['b_rel0'], 'L1_gnn_W_root0': _L1_gnn_in['W_root0'], 'L1_gnn_W_rel1': _L1_gnn_in['W_rel1'], 'L1_gnn_b_rel1': _L1_gnn_in['b_rel1'], 'L1_gnn_W_root1': _L1_gnn_in['W_root1']}

def reference(x, src, dst, edge_attr_64, edge_weight, L0_gnn_We1, L0_gnn_be1, L0_gnn_We2, L0_gnn_be2, L0_gnn_Wt, L0_gnn_bt, L0_gnn_Wn1, L0_gnn_bn1, L0_gnn_Wn2, L0_gnn_bn2, L1_gnn_W_rel0, L1_gnn_b_rel0, L1_gnn_W_root0, L1_gnn_W_rel1, L1_gnn_b_rel1, L1_gnn_W_root1):
    import jax
    import jax.numpy as jnp

    def _L0_gnn_ref(x, edge_index, edge_attr, timestamps, We1, be1, We2, be2, Wt, bt, Wn1, bn1, Wn2, bn2):
        import jax, jax.numpy as jnp
        import numpy as np
        N_NODES = 12500
        N_EDGES = 62500
        IN_CH = 128
        EDGE_CH = 64

        def _glorot(key, shape):
            fan_in, fan_out = (shape[0], shape[1])
            lim = (6.0 / (fan_in + fan_out)) ** 0.5
            return jax.random.uniform(key, shape, jnp.float32, -lim, lim)
        ts = timestamps[:, None]
        ef = jax.nn.relu(edge_attr @ We1 + be1) @ We2 + be2
        tw = jax.nn.sigmoid(ts @ Wt + bt)
        ef = ef * tw
        row, col = (edge_index[0], edge_index[1])
        combined = jnp.concatenate([x[row], ef], axis=1)
        msg = jax.nn.relu(combined @ Wn1 + bn1) @ Wn2 + bn2
        out = jax.ops.segment_sum(msg, col, num_segments=x.shape[0])
        return out + x

    def _L1_gnn_ref(x, edge_index, W_rel0, b_rel0, W_root0, W_rel1, b_rel1, W_root1):
        import jax, jax.numpy as jnp
        import numpy as np
        N_NODES = 6250
        N_EDGES = 62500
        D = 128
        n = x.shape[0]
        src = edge_index[0]
        dst = edge_index[1]
        deg = jax.ops.segment_sum(jnp.ones_like(dst, dtype=x.dtype), dst, num_segments=n)
        inv_deg = 1.0 / jnp.maximum(deg, 1.0)
        layers = [(W_rel0, b_rel0, W_root0), (W_rel1, b_rel1, W_root1)]
        num_layers = len(layers)
        for i, (Wr, br, Wo) in enumerate(layers):
            msgs = x[src]
            agg = jax.ops.segment_sum(msgs, dst, num_segments=n) * inv_deg[:, None]
            x = agg @ Wr + br + x @ Wo
            if i != num_layers - 1:
                x = jax.nn.relu(x)
        return x
    edge_index = jnp.stack([src, dst])
    x = _layernorm(x + _L0_gnn_ref(x, edge_index, edge_attr_64, edge_weight, L0_gnn_We1, L0_gnn_be1, L0_gnn_We2, L0_gnn_be2, L0_gnn_Wt, L0_gnn_bt, L0_gnn_Wn1, L0_gnn_bn1, L0_gnn_Wn2, L0_gnn_bn2), axis=-1)
    x = _layernorm(x + _L1_gnn_ref(x, edge_index, L1_gnn_W_rel0, L1_gnn_b_rel0, L1_gnn_W_root0, L1_gnn_W_rel1, L1_gnn_b_rel1, L1_gnn_W_root1), axis=-1)
    return x

_drawn_inputs = setup_inputs


def setup_inputs(seed=0):
    import zlib

    import numpy as np

    out = dict(_drawn_inputs(seed))
    spreads = {'L0_gnn_be1': (0.0, 0.1),
     'L0_gnn_be2': (0.0, 0.1),
     'L0_gnn_bt': (0.0, 0.65),
     'L0_gnn_bn1': (0.0, 0.1),
     'L0_gnn_bn2': (0.0, 0.1),
     'L1_gnn_b_rel0': (0.0, 0.1),
     'L1_gnn_b_rel1': (0.0, 0.1)}
    factors = {'edge_weight': 8.0, 'L0_gnn_Wt': 8.0}
    for name, (base, spread) in spreads.items():
        noise = np.random.default_rng([zlib.crc32(name.encode()), seed]).standard_normal(out[name].shape)
        drawn = base * np.exp(spread * noise) if base else spread * noise
        out[name] = jnp.asarray(drawn.astype(out[name].dtype))
    for name, factor in factors.items():
        out[name] = (out[name] * factor).astype(out[name].dtype)
    return out
```

```python
import concourse.bass as bass
from concourse import mybir
from contextlib import ExitStack


def gnn_program(nc, x, src, dst, edge_attr, edge_time, We1, be1, We2, be2, Wt, bt, Wn1, bn1, Wn2, bn2,
                Wr0, br0, Wo0, Wr1, br1, Wo1, out):
    f32, bf16, i32 = mybir.dt.float32, mybir.dt.bfloat16, mybir.dt.int32
    ALU, ACT, AX = mybir.AluOpType, mybir.ActivationFunctionType, mybir.AxisListType

    P = 128
    N, F = x.shape
    E, CH = edge_attr.shape
    NT = -(-N // P)
    NP = NT * P
    WN = P
    NWIN = NP // WN
    TPG = 4
    GE = TPG * P
    NG = -(-E // GE)
    LAST = E - GE
    REPEATED = NG * GE - E
    U = 4
    assert NG % U == 0 and F == P
    HALVES = 2
    CT = 7
    NCH = NT // CT
    CN = CT * P
    assert NCH * CT == NT and NCH == 7
    TAIL = N - (NT - 1) * P
    EPS = 1e-5
    NOWHERE = float(1 << 20)
    NPH = 3

    table = [nc.dram_tensor(f"table{i}", (NP, F), f32, kind="Internal").ap() for i in range(NPH)]

    ctx = ExitStack()
    with ctx:
        def sb(name, shape, dt=f32):
            return ctx.enter_context(nc.sbuf_tensor(name, shape, dt))

        def bank(name):
            return ctx.enter_context(nc.psum_tensor(name, [P, 512], f32))

        def sem(name):
            return ctx.enter_context(nc.semaphore(name))

        we1, we2 = sb("we1", [CH, P]), sb("we2", [P, P])
        wn1, wn2 = sb("wn1", [P, 2, P]), sb("wn2", [P, P])
        wr = [sb("wr0", [P, P]), sb("wr1", [P, P])]
        wo = [sb("wo0", [P, P]), sb("wo1", [P, P])]
        cols = sb("cols", [P, 7])
        be1_c, be2_c, wt_c, bt_c, bn2_c = (cols[:, i:i + 1] for i in range(5))
        br_c = [cols[:, 5:6], cols[:, 6:7]]
        bn1_rows = sb("bn1_rows", [P, P])
        ident = sb("ident", [P, P])
        iota = sb("iota", [P, WN])
        win_base = sb("win_base", [P, NWIN])
        ones = sb("ones", [P, P])
        ones16 = sb("ones16", [P, P], bf16)

        acc_a, acc_b, degree = sb("acc_a", [P, NP]), sb("acc_b", [P, NP]), sb("degree", [P, NP])
        x1T = sb("x1T", [P, NP])
        acc = [acc_a, acc_b, acc_a]
        x2T = acc_b

        GC = HALVES * P * TPG
        dst_abs, dst_rel, src_idx = sb("dst_abs", [P, GC]), sb("dst_rel", [P, GC]), sb("src_idx", [P, GC], i32)
        base_row = sb("base_row", [1, HALVES * P], i32)
        flag = sb("flag", [1, 1], i32)
        prep = x1T[:, 0:4 * HALVES * GE].rearrange("p (a h e) -> p a h e", a=4, h=HALVES)
        dst_i, src_i = prep[:, 0].bitcast(i32), prep[:, 1].bitcast(i32)
        dst_g, src_g = prep[:, 2], prep[:, 3]
        lo, hi, base, over = (sb(n, [P, HALVES]) for n in ("lo", "hi", "base", "over"))
        over1, over_f = sb("over1", [P, 1]), sb("over_f", [1, 1])
        diag = sb("diag", [P, HALVES, P])

        ea = sb("ea", [P, U, TPG, CH])
        tsb = sb("tsb", [P, U, GE])
        eaT, h1, tw, efT = sb("eaT", [CH, 2, GE]), sb("h1", [P, 2, GE]), sb("tw", [P, 2, GE]), sb("efT", [P, 2, GE])
        idx = sb("idx", [P, U, TPG], i32)
        rows = sb("rows", [P, U, TPG, F])
        msg = sb("msg", [P, 2, TPG, F])
        onehot = sb("onehot", [P, 2, TPG, WN])
        rel_w = sb("rel_w", [P, TPG])

        xs = sb("xs", [P, 2, CT, F])
        fm = sb("fm", [P, 2, CN])
        nm = sb("nm", [P, 2, CT, F])
        agg = sb("agg", [P, CN])
        inv = sb("inv", [P, CN])
        stats, mv = sb("stats", [P, CT, 6]), sb("mv", [P, CT, 2])
        std, rstd = sb("std", [P, CT]), sb("rstd", [P, CT])
        eps_c = sb("eps_c", [P, 1])

        B = [bank(f"bank{i}") for i in range(8)]
        ps_t, ps_h, ps_e, ps_z, ps_s, ps_d = B[:6]
        def pair(i, rows_=P):
            return [B[2 * i], B[2 * i + 1]]
        SPAN = [(0, 4), (4, CT)]

        def tiles_of(t):
            return slice(SPAN[t][0] * P, SPAN[t][1] * P)

        s = {n: sem(n) for n in (
            "weights", "edges", "edge_pads", "consts", "ident_zero", "zeroed", "prep", "prep_pe", "masked", "lists_ready",
            "idx_ready", "t_done", "a_done", "m1_done", "h_done", "m2_done", "sig_done", "b_done", "m3_done",
            "c_done", "r_done", "oh_done", "seg_done", "acc_done", "gen_rel", "gen_oh", "gen_seg", "gen_acc",
            "xs_free", "fm_ready", "front_done", "tr_done", "nm_ready", "chain", "std_ready", "back_done",
            "x1T_done", "agg_ready", "fmc", "acc_clear", "out_stored", "passed_SP", "passed_Pool", "passed_PE", "passed_DVE")}
        ea_in = [sem(f"ea_in{u}") for u in range(U)]
        ts_in = [sem(f"ts_in{u}") for u in range(U)]
        gathered = [sem(f"gathered{u}") for u in range(U)]
        xs_in = [sem(f"xs_in{u}") for u in range(2)]
        stored = [sem(f"stored{u}") for u in range(2)]

        def wait(eng, semaphore, value):
            if not isinstance(value, int) or value > 0:
                eng.wait_ge(semaphore, value)

        def wait_alone(eng, semaphore, value):
            wait(eng, semaphore, value)
            if not isinstance(value, int):
                eng.sem_inc(s["passed_" + str(eng.engine).split(".")[-1]], 1)

        def over_chunks(eng, body):
            body(0, 0)
            body(1, 1)
            with eng.Fori(1, NCH // 2) as i:
                body(2 * i, 0)
                body(2 * i + 1, 1)
            body(NCH - 1, 0)

        def over_steps(eng, step, lags):
            for k in range(2 * U):
                step(k, k % U, k)
            with eng.Fori(2, NG // U) as i:
                for u in range(U):
                    step(i * U + u, u, i)
            for k in range(NG, NG + lags):
                step(k, k % U, k)

        def has(k, lag):
            return not isinstance(k, int) or 0 <= k - lag < NG

        def uses(k, lag, phase=0):
            if isinstance(k, int):
                return phase * (NG // U) + (k - lag) // U + 1
            return None

        def slot_uses(n, c, u):
            per = (NCH + 1 - u) // 2
            return n * per + (c - u) // 2 + 1 if isinstance(c, int) else None

        block = ctx.enter_context(nc.Block())

        @block.sync
        def _(sp):
            cursor = [0]

            def one(dst_ap, src_ap, semaphore):
                sp.dma_start(dst_ap, src_ap).then_inc(semaphore, 16)

            sp.wait_ge(s["edge_pads"], 2)
            full = (NG - 1 - P) // 64 * 64
            for to, frm in ((dst_i, dst), (src_i, src)):
                one(to[:, 0, :], frm[0:P * GE].rearrange("(q e) -> q e", e=GE), s["edges"])
                one(to[0:full, 1, :], frm[P * GE:(P + full) * GE].rearrange("(q e) -> q e", e=GE), s["edges"])
                one(to[full:NG - 1 - P, 1, :], frm[(P + full) * GE:(NG - 1) * GE].rearrange("(q e) -> q e", e=GE), s["edges"])
                one(to[NG - 1 - P:NG - P, 1, :], frm[LAST:E].rearrange("(q e) -> q e", e=GE), s["edges"])
            one(wn1[:, :, :], Wn1.rearrange("(a k) n -> k a n", a=2), s["weights"])
            one(bn1_rows[:, :], bn1.rearrange("(a n) -> a n", a=1).to_broadcast((P, P)), s["weights"])
            for w, d in ((we1, We1), (we2, We2), (wn2, Wn2), (wr[0], Wr0), (wr[1], Wr1), (wo[0], Wo0), (wo[1], Wo1)):
                one(w[:, :], d, s["weights"])
            for i, v in enumerate((be1, be2, None, bt, bn2, br0, br1)):
                one(cols[:, i:i + 1], Wt.rearrange("a n -> n a") if v is None else v.rearrange("(n a) -> n a", a=1), s["weights"])

            def load_rows(frm, n, c, u, rows_in):
                first = c * CN
                if isinstance(c, int) and c == NCH - 1 and rows_in < NP:
                    sp.dma_start(xs[:, u, 0:CT - 1, :],
                                 frm[first:first + (CT - 1) * P, :].rearrange("(t p) f -> p t f", p=P)).then_inc(xs_in[u], 16)
                    sp.dma_start(xs[0:TAIL, u, CT - 1, :], frm[N - TAIL:N, :]).then_inc(xs_in[u], 16)
                else:
                    sp.dma_start(xs[:, u, :, :],
                                 frm[bass.ds(first, CN), :].rearrange("(t p) f -> p t f", p=P)).then_inc(xs_in[u], 32)

            def store_rows(to, c, u):
                first = c * CN
                sp.dma_start(to[bass.ds(first, CN), :].rearrange("(t p) f -> p t f", p=P), nm[:, u, :, :]).then_inc(stored[u], 16)

            load_rows(x, 0, 0, 0, N)
            load_rows(x, 0, 1, 1, N)

            def nodes0(c, u):
                wait(sp, s["nm_ready"], c + 1)
                store_rows(table[0], c, u)
                if isinstance(c, int) and c + 2 < NCH or not isinstance(c, int):
                    sp.wait_ge(s["fm_ready"], c + 1)
                    load_rows(x, 0, c + 2, u, N)
            body0 = nodes0
            nodes0(0, 0)
            nodes0(1, 1)
            with sp.Fori(1, 2) as i:
                nodes0(2 * i, 0)
                nodes0(2 * i + 1, 1)
            nodes0(4, 0)
            nodes0(5, 1)
            nodes0(6, 0)

            def edges(g, u, i):
                wait(sp, s["t_done"], g - U + 1)
                first = LAST if isinstance(g, int) and g == NG - 1 else g * GE
                sp.dma_start(ea[:, u, :, :], edge_attr[bass.ds(first, GE), :].rearrange("(p j) c -> p j c", j=TPG)).then_inc(ea_in[u], 16)
                wait_alone(sp, s["sig_done"], g - U + 1)
                sp.dma_start(tsb[:, u, :], edge_time[bass.ds(first, GE)].rearrange("(a e) -> a e", a=1).to_broadcast((P, GE))).then_inc(ts_in[u], 16)
            for g in range(U):
                edges(g, g, g)
            with sp.Fori(1, NG // U - 1) as i:
                for u in range(U):
                    edges(i * U + u, u, i)
            for g in range(NG - U, NG):
                edges(g, g % U, g)

            for n, frm, to in ((1, x, table[1]), (2, None, table[2]), (3, table[1], out)):
                if frm is not None:
                    k = {1: 1, 3: 2}[n]
                    sp.wait_ge(s["xs_free"], NCH) if n == 3 else sp.wait_ge(s["fm_ready"], NCH)
                    load_rows(frm, k, 0, 0, frm.shape[0])
                    load_rows(frm, k, 1, 1, frm.shape[0])

                def step(c, u, n=n, frm=frm, to=to):
                    sp.wait_ge(s["nm_ready"], n * NCH + c + 1)
                    if n == 3 and isinstance(c, int) and c == NCH - 1:
                        sp.dma_start(out[c * CN:c * CN + (CT - 1) * P, :].rearrange("(t p) f -> p t f", p=P),
                                     nm[:, u, 0:CT - 1, :]).then_inc(s["out_stored"], 16)
                        sp.dma_start(out[N - TAIL:N, :], nm[0:TAIL, u, CT - 1, :]).then_inc(s["out_stored"], 16)
                    elif n == 3:
                        sp.dma_start(out[bass.ds(c * CN, CN), :].rearrange("(t p) f -> p t f", p=P), nm[:, u, :, :]).then_inc(stored[u], 16)
                    else:
                        store_rows(to, c, u)
                    if frm is not None and (not isinstance(c, int) or c + 2 < NCH):
                        sp.wait_ge(s["xs_free"], NCH * {1: 0, 3: 1}[n] + c + 1)
                        load_rows(frm, n, c + 2, u, frm.shape[0])
                step(0, 0)
                step(1, 1)
                with sp.Fori(1, 2) as i:
                    step(2 * i, 0)
                    step(2 * i + 1, 1)
                step(4, 0)
                step(5, 1)
                step(6, 0)
            sp.wait_ge(stored[0], 16 * (4 * 4 - 1))
            sp.wait_ge(stored[1], 16 * 4 * 3)
            sp.wait_ge(s["out_stored"], 32)

        @block.gpsimd
        def _(pool):
            nc.gpsimd.memset(dst_i[:, 1, :], 0).then_inc(s["edge_pads"], 1)
            nc.gpsimd.memset(src_i[:, 1, :], 0).then_inc(s["edge_pads"], 1)
            nc.gpsimd.memset(ident[:, :], 0.0).then_inc(s["ident_zero"], 1)
            pool.wait_ge(s["ident_zero"], 1)
            nc.gpsimd.affine_select(out=ident[:, :], in_=ident[:, :], compare_op=ALU.not_equal, fill=1.0, base=0,
                                    pattern=[[-1, P]], channel_multiplier=1).then_inc(s["consts"], 1)
            nc.gpsimd.memset(ones[:, :], 1.0).then_inc(s["consts"], 1)
            nc.gpsimd.memset(ones16[:, :], 1.0).then_inc(s["consts"], 1)
            nc.gpsimd.iota(iota[:, :], pattern=[[1, WN]], base=0, channel_multiplier=0,
                           allow_small_or_imprecise_dtypes=True).then_inc(s["consts"], 1)
            nc.gpsimd.iota(win_base[:, :], pattern=[[WN, NWIN]], base=0, channel_multiplier=0,
                           allow_small_or_imprecise_dtypes=True).then_inc(s["consts"], 1)
            nc.gpsimd.memset(eps_c[:, :], EPS).then_inc(s["consts"], 1)
            for a in (acc_a, acc_b, degree):
                nc.gpsimd.memset(a[:, :], 0.0).then_inc(s["zeroed"], 1)
            pool.wait_ge(s["prep"], 1)
            q = NG - 1 - P
            nc.gpsimd.affine_select(out=dst_g[:, 1, :], in_=dst_g[:, 1, :], compare_op=ALU.is_ge, fill=NOWHERE,
                                    base=GE * 2 * q - REPEATED, pattern=[[1, GE]], channel_multiplier=-GE * 2).then_inc(s["masked"], 1)

            for ph in range(NPH):
                pool.wait_ge(stored[0], 16 * 4 * (ph + 1))
                pool.wait_ge(stored[1], 16 * 3 * (ph + 1))

                def group(g, u, i, ph=ph):
                    pool.wait_ge(s["idx_ready"], ph * NG + g + 1)
                    if ph == 0:
                        wait_alone(pool, s["c_done"], g - U + 1)
                    elif not isinstance(g, int) or g >= U:
                        wait_alone(pool, s["seg_done"], ph * NG + g - U + 1)
                    for j in range(TPG):
                        nc.gpsimd.indirect_dma_start(
                            rows[:, u, j, :], None, table[ph][:, :],
                            bass.IndirectOffsetOnAxis(ap=idx[:, u, j:j + 1], axis=0)).then_inc(gathered[u], 16)
                for g in range(U):
                    group(g, g, 0)
                with pool.Fori(1, NG // U) as i:
                    for u in range(U):
                        group(i * U + u, u, i)

        @block.scalar
        def _(act):
            def stage_idx(ph, g, u, i):
                if not (isinstance(g, int) and g < U):
                    before = ph * (NG // U) + (g // U if isinstance(g, int) else i)
                    act.wait_ge(gathered[u], 16 * TPG * before)
                nc.scalar.copy(idx[:, u, :], src_idx[:, bass.ds(g * TPG, TPG)]).then_inc(s["idx_ready"], 1)

            act.wait_ge(s["weights"], 16 * 16)
            act.wait_ge(s["lists_ready"], 1)

            def nodes0(c, u):
                act.wait_ge(s["front_done"], c + 1)
                wait(act, s["fmc"], c - 1)
                for t in range(2):
                    last = nc.scalar.copy(fm[:, u, tiles_of(t)], pair(0)[t][:, 0:(SPAN[t][1] - SPAN[t][0]) * P])
                last.then_inc(s["fm_ready"], 1)
            over_chunks(act, nodes0)

            def step(k, u, i):
                if has(k, 0):
                    stage_idx(0, k, u, i)
                if has(k, 1):
                    g = k - 1
                    act.wait_ge(s["m1_done"], g + 1)
                    wait(act, s["m2_done"], g - 1)
                    nc.scalar.activation(h1[:, (u - 1) % 2, :], ps_h[:, :], ACT.Relu, bias=be1_c).then_inc(s["h_done"], 1)
                if has(k, 2):
                    g = k - 2
                    v = (u - 2) % U
                    use = g // U + 1 if isinstance(g, int) else (i + 1 if u >= 2 else i)
                    act.wait_ge(ts_in[v], 16 * use)
                    wait(act, s["b_done"], g - 1)
                    nc.scalar.activation(tw[:, v % 2, :].rearrange("f (j p) -> f j p", j=TPG),
                                         tsb[:, v, :].rearrange("f (p j) -> f j p", j=TPG),
                                         ACT.Sigmoid, scale=wt_c, bias=bt_c).then_inc(s["sig_done"], 1)
                if has(k, 3):
                    g = k - 3
                    act.wait_ge(s["c_done"], g + 1)
                    m = msg[:, (u - 3) % 2, :, :]
                    nc.scalar.activation(m, m, ACT.Relu).then_inc(s["r_done"], 1)
            over_steps(act, step, 5)

            def nodes1(c, u):
                act.wait_ge(s["chain"], 3 * (c + 1) - 1)
                nc.scalar.activation(std[:, :], mv[:, :, 1], ACT.Sqrt, bias=eps_c[:, :]).then_inc(s["std_ready"], 1)
                act.wait_ge(s["back_done"], c + 1)
                for t in range(2):
                    last = nc.scalar.copy(x1T[:, bass.ds(c * CN + SPAN[t][0] * P, (SPAN[t][1] - SPAN[t][0]) * P)],
                                          pair(2)[t][:, 0:(SPAN[t][1] - SPAN[t][0]) * P])
                last.then_inc(s["x1T_done"], 1)
            over_chunks(act, nodes1)

            for ph in (1, 2):
                for g in range(U):
                    act.wait_ge(gathered[g], 16 * TPG * ph * (NG // U))
                    nc.scalar.copy(idx[:, g, :], src_idx[:, g * TPG:(g + 1) * TPG]).then_inc(s["idx_ready"], 1)
                with act.Fori(1, NG // U) as i:
                    for u in range(U):
                        stage_idx(ph, i * U + u, u, i)

                def nodes(c, u, ph=ph):
                    done = (ph - 1) * NCH + c + 1
                    act.wait_ge(s["front_done"], (ph + 1) * NCH + c + 1)
                    wait(act, s["tr_done"], ph * NCH + c - 1)
                    for t in range(2):
                        last = nc.scalar.activation(fm[:, u, tiles_of(t)], pair(0)[t][:, 0:(SPAN[t][1] - SPAN[t][0]) * P],
                                                    ACT.Relu if ph == 1 else ACT.Identity, bias=br_c[ph - 1])
                    last.then_inc(s["fm_ready"], 1)
                    if ph == 1:
                        act.wait_ge(s["fm_ready"], (ph + 1) * NCH + c + 1)
                        nc.scalar.copy(x2T[:, bass.ds(c * CN, CN)], fm[:, u, :]).then_inc(s["x1T_done"], 1)
                    else:
                        act.wait_ge(s["chain"], 3 * (NCH + c + 1) - 1)
                        nc.scalar.activation(std[:, :], mv[:, :, 1], ACT.Sqrt, bias=eps_c[:, :]).then_inc(s["std_ready"], 1)
                over_chunks(act, nodes)

        @block.tensor
        def _(pe):
            def transposes(dst_banks, src_of):
                for t in range(2):
                    for j in range(*SPAN[t]):
                        o = (j - SPAN[t][0]) * P
                        last = nc.tensor.transpose(dst_banks[t][:, o:o + P], src_of(j), ident[:, :])
                return last

            pe.wait_ge(s["consts"], 6)
            pe.wait_ge(s["prep"], 2)
            nc.tensor.transpose(B[6][0:1, 0:P], over1[:, :], ident[:, :])
            for h in range(HALVES):
                nc.tensor.transpose(B[6][0:1, (h + 1) * P:(h + 2) * P], base[:, h:h + 1], ident[:, :])
            for h in range(HALVES):
                last = nc.tensor.matmul(B[7][:, h * P:(h + 1) * P], ones[:, :], diag[:, h, :], start=True, stop=True)
            pe.wait_ge(s["masked"], 1)
            for n, lists in enumerate((dst_g, src_g)):
                for h in range(HALVES):
                    for j in range(TPG):
                        v = lists[:, h, :].rearrange("q (p j) -> q j p", j=TPG)[:, j, :]
                        last = nc.tensor.transpose(B[2 * n + h][:, j * P:(j + 1) * P], v, ident[:, :])
            last.then_inc(s["prep_pe"], 1)
            pe.wait_ge(s["weights"], 16 * 16)
            pe.wait_ge(s["lists_ready"], 1)

            def nodes0(c, u):
                use = c // 2 + 1 if isinstance(c, int) else i_of(c, u)
                pe.wait_ge(xs_in[u], 32 * use)
                wait(pe, s["fm_ready"], c)
                transposes(pair(0), lambda j: xs[:, u, j, :]).then_inc(s["front_done"], 1)
                pe.wait_ge(s["fm_ready"], c + 1)
                wait(pe, s["nm_ready"], c)
                for t in range(2):
                    for j in range(*SPAN[t]):
                        o = (j - SPAN[t][0]) * P
                        last = nc.tensor.matmul(pair(1)[t][:, o:o + P], fm[:, u, j * P:(j + 1) * P], wn1[:, 0, :],
                                                start=True, stop=True)
                last.then_inc(s["fmc"], 1)

            holder = {}

            def i_of(c, u):
                return holder["i"] + 1

            nodes0(0, 0)
            nodes0(1, 1)
            with pe.Fori(1, NCH // 2) as i:
                holder["i"] = i
                nodes0(2 * i, 0)
                nodes0(2 * i + 1, 1)
            nodes0(NCH - 1, 0)
            pe.wait_ge(s["nm_ready"], NCH)

            def segment_sum(ph, k, lag, u, i, general):
                g = k - lag
                v = (u - lag) % U
                seq = ph * NG + g
                if ph == 0:
                    wait_alone(pe, s["r_done"], g + 1)
                    data = msg[:, v % 2, :, :]
                else:
                    use = ph * (NG // U) + (g // U + 1 if isinstance(g, int) else (i + 1))
                    wait_alone(pe, gathered[v], 16 * TPG * use)
                    data = rows[:, v, :, :]

                def window(oh, signal):
                    for j in range(TPG):
                        last = nc.tensor.matmul(ps_s[:, 0:WN], data[:, j, :], oh[:, j, :], start=(j == 0), stop=(j == TPG - 1))
                        if ph == 0:
                            half = oh[:, j, :].bitcast(bf16).rearrange("p (n t) -> p t n", t=2)[:, 1, :]
                            last = nc.tensor.matmul(ps_d[:, 0:WN], ones16[:, :], half, start=(j == 0), stop=(j == TPG - 1))
                    last.then_inc(signal, 1)
                if general:
                    oh = onehot[:, 0, :, :]
                    with pe.Fori(0, NWIN - 1) as w:
                        pe.wait_ge(s["gen_oh"], seq * NWIN + w + 1)
                        window(oh, s["gen_seg"])
                    pe.wait_ge(s["gen_oh"], seq * NWIN + NWIN)
                    window(oh, s["seg_done"])
                else:
                    pe.wait_ge(s["oh_done"], seq + 1)
                    wait(pe, s["acc_done"], seq)
                    window(onehot[:, v % 2, :, :], s["seg_done"])

            def step_of(general):
                def step(k, u, i):
                    if has(k, 0):
                        use = k // U + 1 if isinstance(k, int) else i + 1
                        pe.wait_ge(ea_in[u], 16 * use)
                        wait_alone(pe, s["a_done"], k)
                        for j in range(TPG):
                            last = nc.tensor.transpose(ps_t[0:CH, j * P:(j + 1) * P], ea[:, u, j, :], ident[:, :])
                        last.then_inc(s["t_done"], 1)
                    if has(k, 1):
                        g = k - 1
                        pe.wait_ge(s["a_done"], g + 1)
                        wait(pe, s["h_done"], g)
                        nc.tensor.matmul(ps_h[:, :], we1[:, :], eaT[:, (u - 1) % 2, :], start=True, stop=True).then_inc(s["m1_done"], 1)
                    if has(k, 2):
                        g = k - 2
                        pe.wait_ge(s["h_done"], g + 1)
                        wait(pe, s["b_done"], g)
                        nc.tensor.matmul(ps_e[:, :], we2[:, :], h1[:, (u - 2) % 2, :], start=True, stop=True).then_inc(s["m2_done"], 1)
                    if has(k, 3):
                        g = k - 3
                        pe.wait_ge(s["b_done"], g + 1)
                        wait(pe, s["c_done"], g)
                        for j in range(TPG):
                            last = nc.tensor.matmul(ps_z[:, j * P:(j + 1) * P], efT[:, (u - 3) % 2, j * P:(j + 1) * P],
                                                    wn1[:, 1, :], start=True, stop=True)
                        last.then_inc(s["m3_done"], 1)
                    if has(k, 4):
                        segment_sum(0, k, 4, u, i, general)
                return step

            def front(ph):
                def chunk(c, u):
                    a = acc[ph]
                    wait(pe, s["nm_ready"] if ph == 0 else s["fm_ready"], (ph + 1) * NCH + c)
                    if ph == 0:
                        for t in range(2):
                            width = (SPAN[t][1] - SPAN[t][0]) * P
                            last = nc.tensor.matmul(pair(0)[t][:, 0:width], wn2[:, :],
                                                    a[:, bass.ds(c * CN + SPAN[t][0] * P, width)], start=True, stop=True)
                    else:
                        pe.wait_ge(s["agg_ready"], (ph - 1) * NCH + c + 1)
                        other = x1T if ph == 1 else x2T
                        for t in range(2):
                            width = (SPAN[t][1] - SPAN[t][0]) * P
                            nc.tensor.matmul(pair(0)[t][:, 0:width], wr[ph - 1][:, :], agg[:, tiles_of(t)], start=True, stop=False)
                            last = nc.tensor.matmul(pair(0)[t][:, 0:width], wo[ph - 1][:, :],
                                                    other[:, bass.ds(c * CN + SPAN[t][0] * P, width)], start=False, stop=True)
                    last.then_inc(s["front_done"], 1)
                    pe.wait_ge(s["fm_ready"], (ph + 1) * NCH + c + 1)
                    pe.wait_ge(s["nm_ready"], (ph + 1) * NCH + c) if not (isinstance(c, int) and c == 0) else None
                    transposes(pair(1), lambda j: fm[:, u, j * P:(j + 1) * P]).then_inc(s["tr_done"], 1)
                    if ph == 0:
                        pe.wait_ge(s["nm_ready"], NCH + c + 1)
                        wait(pe, s["x1T_done"], c)
                        transposes(pair(2), lambda j: nm[:, u, j, :]).then_inc(s["back_done"], 1)
                return chunk

            def all_phases(general):
                over_steps(pe, step_of(general), 5)
                pe.wait_ge(s["acc_done"], NG)
                over_chunks(pe, front(0))
                for ph in (1, 2):
                    for g in range(U):
                        segment_sum(ph, g, 0, g, 0, general)
                    with pe.Fori(1, NG // U) as i:
                        for u in range(U):
                            segment_sum(ph, i * U + u, 0, u, i, general)
                    pe.wait_ge(s["x1T_done"], NCH * ph)
                    over_chunks(pe, front(ph))

            spread = pe.value_load(flag[0:1, 0:1], min_val=0, max_val=1)
            with pe.If(spread == 0):
                all_phases(False)
            with pe.Else():
                all_phases(True)

        @block.vector
        def _(dve):
            steps = [0]

            def link(ins):
                steps[0] += 1
                ins.then_inc(s["gen_rel"], 1)
                dve.wait_ge(s["gen_rel"], steps[0])

            dve.wait_ge(s["edges"], 16 * 8)
            link(nc.vector.tensor_copy(dst_g[:, :, :], dst_i[:, :, :]))
            nc.vector.tensor_copy(src_g[:, :, :], src_i[:, :, :])
            nc.vector.tensor_reduce(lo[:, :], dst_g[:, :, :], AX.X, ALU.min)
            nc.vector.tensor_reduce(hi[:, :], dst_g[:, :, :], AX.X, ALU.max).then_inc(s["prep"], 1)
            dve.wait_ge(s["prep"], 1)
            link(nc.vector.tensor_scalar(base[:, :], lo[:, :], float(NP - WN), None, ALU.min))
            link(nc.vector.tensor_tensor(over[:, :], hi[:, :], base[:, :], ALU.subtract))
            link(nc.vector.tensor_reduce(over1[:, :], over[:, :], AX.X, ALU.max))
            dve.wait_ge(s["consts"], 6)
            for h in range(HALVES):
                last = nc.vector.tensor_scalar(diag[:, h, :], ident[:, :], base[:, h:h + 1], None, ALU.mult)
            last.then_inc(s["prep"], 1)
            dve.wait_ge(s["prep_pe"], 1)
            link(nc.vector.tensor_reduce(over_f[:, :], B[6][0:1, 0:P], AX.X, ALU.max))
            nc.vector.tensor_scalar(flag[:, :], over_f[:, :], float(WN), None, ALU.is_ge)
            nc.vector.tensor_copy(base_row[:, :], B[6][0:1, P:(1 + HALVES) * P])
            for h in range(HALVES):
                to = dst_abs[:, h * P * TPG:(h + 1) * P * TPG].rearrange("p (q j) -> p q j", j=TPG)
                nc.vector.tensor_copy(to, B[h][:, :].rearrange("p (j q) -> p q j", j=TPG))
                to = src_idx[:, h * P * TPG:(h + 1) * P * TPG].rearrange("p (q j) -> p q j", j=TPG)
                last = nc.vector.tensor_copy(to, B[2 + h][:, :].rearrange("p (j q) -> p q j", j=TPG))
            link(last)
            for h in range(HALVES):
                to, frm = (a[:, h * P * TPG:(h + 1) * P * TPG].rearrange("p (q j) -> p q j", j=TPG) for a in (dst_rel, dst_abs))
                for j in range(TPG):
                    last = nc.vector.tensor_tensor(to[:, :, j], frm[:, :, j], B[7][:, h * P:(h + 1) * P], ALU.subtract)
            last.then_inc(s["lists_ready"], 1)
            dve.wait_ge(s["lists_ready"], 1)
            dve.wait_ge(s["weights"], 16 * 16)

            def nodes0(c, u):
                dve.wait_ge(s["fmc"], c + 1)
                if not isinstance(c, int) or c >= 2:
                    dve.wait_ge(stored[u], 16 * (holder["i"] if not isinstance(c, int) else c // 2))
                for t in range(2):
                    a, b = SPAN[t]
                    last = nc.vector.tensor_tensor(nm[:, u, a:b, :], pair(1)[t][:, 0:(b - a) * P].rearrange("p (t f) -> p t f", f=F),
                                                   bn1_rows[:, None, :].to_broadcast((P, b - a, F)), ALU.add)
                last.then_inc(s["nm_ready"], 1)

            holder = {}

            def chunks(body):
                body(0, 0)
                body(1, 1)
                with dve.Fori(1, NCH // 2) as i:
                    holder["i"] = i
                    body(2 * i, 0)
                    body(2 * i + 1, 1)
                body(NCH - 1, 0)
            chunks(nodes0)
            dve.wait_ge(s["zeroed"], 3)

            def one_hots(seq, cols_ap, v, signal):
                for j in range(TPG):
                    last = nc.vector.tensor_scalar(onehot[:, v, j, :], iota[:, :], cols_ap(j), None, ALU.is_equal)
                last.then_inc(signal, 1)

            def fast_one_hots(ph, g, v):
                wait(dve, s["seg_done"], ph * NG + g - 1)
                one_hots(None, lambda j: dst_rel[:, bass.ds(g * TPG + j, 1)], v % 2, s["oh_done"])

            def fast_add(ph, g, at):
                seq = ph * NG + g
                dve.wait_ge(s["seg_done"], seq + 1)
                wait(dve, s["acc_done"], seq)
                if ph == 0:
                    o = degree[:, bass.ds(at, WN)]
                    nc.vector.tensor_tensor(o, o, ps_d[:, 0:WN], ALU.add)
                o = acc[ph][:, bass.ds(at, WN)]
                nc.vector.tensor_tensor(o, o, ps_s[:, 0:WN], ALU.add).then_inc(s["acc_done"], 1)

            def base_of(g):
                return dve.value_load(base_row[0:1, bass.ds(g, 1)], min_val=0, max_val=NP - WN)

            def all_windows(ph, g):
                seq = ph * NG + g

                def window(w, at, signal, value):
                    nc.vector.tensor_scalar(rel_w[:, :], dst_abs[:, bass.ds(g * TPG, TPG)], win_base[:, bass.ds(w, 1)], None,
                                            ALU.subtract).then_inc(s["gen_acc"], 1)
                    dve.wait_ge(s["gen_acc"], 2 * (seq * NWIN + w) + 1)
                    one_hots(None, lambda j: rel_w[:, j:j + 1], 0, s["gen_oh"])
                    dve.wait_ge(signal, value)
                    if ph == 0:
                        o = degree[:, bass.ds(at, WN)]
                        nc.vector.tensor_tensor(o, o, ps_d[:, 0:WN], ALU.add)
                    o = acc[ph][:, bass.ds(at, WN)]
                    nc.vector.tensor_tensor(o, o, ps_s[:, 0:WN], ALU.add).then_inc(s["gen_acc"], 1)
                    dve.wait_ge(s["gen_acc"], 2 * (seq * NWIN + w) + 2)
                with dve.Fori(0, NWIN - 1) as w:
                    window(w, w * WN, s["gen_seg"], seq * (NWIN - 1) + w + 1)
                window(NWIN - 1, (NWIN - 1) * WN, s["seg_done"], seq + 1)
                nc.vector.tensor_copy(rel_w[:, :], iota[:, 0:TPG]).then_inc(s["acc_done"], 1)

            def step_of(general):
                def step(k, u, i):
                    if has(k, 0):
                        dve.wait_ge(s["t_done"], k + 1)
                        wait(dve, s["m1_done"], k - 1)
                        nc.vector.tensor_copy(eaT[:, u % 2, :], ps_t[0:CH, :]).then_inc(s["a_done"], 1)
                    if not general and has(k, 5):
                        fast_add(0, k - 5, base_of(k - 5))
                    if not general and has(k, 3):
                        fast_one_hots(0, k - 3, u - 3)
                    if has(k, 2):
                        g = k - 2
                        dve.wait_ge(s["m2_done"], g + 1)
                        dve.wait_ge(s["sig_done"], g + 1)
                        wait(dve, s["m3_done"], g - 1)
                        nc.vector.scalar_tensor_tensor(out=efT[:, u % 2, :], in0=ps_e[:, :], scalar=be2_c, in1=tw[:, u % 2, :],
                                                       op0=ALU.add, op1=ALU.mult).then_inc(s["b_done"], 1)
                    if has(k, 3):
                        g = k - 3
                        v = (u - 3) % U
                        use = g // U + 1 if isinstance(g, int) else (i + 1 if u == 3 else i)
                        dve.wait_ge(s["m3_done"], g + 1)
                        dve.wait_ge(gathered[v], 16 * TPG * use)
                        wait(dve, s["seg_done"], g - 1)
                        nc.vector.tensor_tensor(msg[:, v % 2, :, :], ps_z[:, :].rearrange("p (j f) -> p j f", j=TPG),
                                                rows[:, v, :, :], ALU.add).then_inc(s["c_done"], 1)
                    if general and has(k, 4):
                        all_windows(0, k - 4)
                return step

            def normalise(c, u, n):
                for j in range(CT):
                    last = nc.vector.bn_stats(stats[:, j, :], nm[:, u, j, :])
                last.then_inc(s["chain"], 1)
                wait_alone(dve, s["chain"], 3 * n + 1)
                for j in range(CT):
                    last = nc.vector.bn_aggr(mv[:, j, :], stats[:, j, :])
                last.then_inc(s["chain"], 1)
                dve.wait_ge(s["std_ready"], n + 1)
                nc.vector.reciprocal(rstd[:, :], std[:, :]).then_inc(s["chain"], 1)
                dve.wait_ge(s["chain"], 3 * n + 3)
                for j in range(CT):
                    last = nc.vector.tensor_scalar(nm[:, u, j, :], nm[:, u, j, :], mv[:, j, 0:1], rstd[:, j:j + 1],
                                                   ALU.subtract, ALU.mult)
                last.then_inc(s["nm_ready"], 1)

            def slot_stored(n, c, u):
                per = 4 - u
                before = c // 2 if isinstance(c, int) else holder["i"]
                dve.wait_ge(stored[u], 16 * (n * per + before))

            def slot_loaded(k, c, u):
                per = 4 - u
                before = c // 2 if isinstance(c, int) else holder["i"]
                dve.wait_ge(xs_in[u], 32 * (k * per + before + 1))

            def nodes1(c, u):
                dve.wait_ge(s["front_done"], NCH + c + 1)
                for t in range(2):
                    a, b = SPAN[t]
                    last = nc.vector.scalar_tensor_tensor(
                        out=fm[:, u, tiles_of(t)], in0=degree[:, bass.ds(c * CN + a * P, (b - a) * P)], scalar=bn2_c,
                        in1=pair(0)[t][:, 0:(b - a) * P], op0=ALU.mult, op1=ALU.add)
                last.then_inc(s["fm_ready"], 1)
                dve.wait_ge(s["tr_done"], c + 1)
                slot_loaded(1, c, u)
                slot_stored(1, c, u)
                for t in range(2):
                    a, b = SPAN[t]
                    last = nc.vector.scalar_tensor_tensor(
                        out=nm[:, u, a:b, :], in0=xs[:, u, a:b, :], scalar=2.0,
                        in1=pair(1)[t][:, 0:(b - a) * P].rearrange("p (t f) -> p t f", f=F), op0=ALU.mult, op1=ALU.add)
                last.then_inc(s["xs_free"], 1)
                dve.wait_ge(s["xs_free"], c + 1)
                normalise(c, u, c)

            def nodes(ph):
                def chunk(c, u):
                    n = (ph - 1) * NCH + c
                    nc.vector.tensor_scalar(inv[:, :], degree[:, bass.ds(c * CN, CN)], 1.0, None, ALU.max).then_inc(s["acc_clear"], 1)
                    dve.wait_ge(s["acc_clear"], 2 * n + 1)
                    nc.vector.reciprocal(inv[:, :], inv[:, :]).then_inc(s["acc_clear"], 1)
                    dve.wait_ge(s["acc_clear"], 2 * n + 2)
                    nc.vector.tensor_tensor(agg[:, :], acc[ph][:, bass.ds(c * CN, CN)], inv[:, :], ALU.mult).then_inc(s["agg_ready"], 1)
                    dve.wait_ge(s["tr_done"], ph * NCH + c + 1)
                    slot_stored(ph + 1, c, u)
                    for t in range(2):
                        a, b = SPAN[t]
                        view = pair(1)[t][:, 0:(b - a) * P].rearrange("p (t f) -> p t f", f=F)
                        if ph == 1:
                            last = nc.vector.tensor_copy(nm[:, u, a:b, :], view)
                        else:
                            if t == 0:
                                slot_loaded(2, c, u)
                            last = nc.vector.tensor_tensor(nm[:, u, a:b, :], xs[:, u, a:b, :], view, ALU.add)
                    if ph == 1:
                        last.then_inc(s["nm_ready"], 1)
                    else:
                        last.then_inc(s["xs_free"], 1)
                        dve.wait_ge(s["xs_free"], NCH + c + 1)
                        normalise(c, u, NCH + c)
                return chunk

            def all_phases(general):
                over_steps(dve, step_of(general), 6)
                dve.wait_ge(s["acc_done"], NG)
                chunks(nodes1)
                dve.wait_ge(s["front_done"], 2 * NCH)
                nc.vector.memset(acc_a[:, :], 0.0).then_inc(s["zeroed"], 1)
                dve.wait_ge(s["zeroed"], 4)
                for ph in (1, 2):
                    if general:
                        with dve.Fori(0, NG) as g:
                            all_windows(ph, g)
                    else:
                        for g in range(U):
                            fast_one_hots(ph, g, g)
                            if g:
                                fast_add(ph, g - 1, base_of(g - 1))
                        with dve.Fori(1, NG // U) as i:
                            for u in range(U):
                                g = i * U + u
                                fast_one_hots(ph, g, u)
                                fast_add(ph, g - 1, base_of(g - 1))
                        fast_add(ph, NG - 1, base_of(NG - 1))
                    dve.wait_ge(s["acc_done"], (ph + 1) * NG)
                    chunks(nodes(ph))

            spread = dve.value_load(flag[0:1, 0:1], min_val=0, max_val=1)
            with dve.If(spread == 0):
                all_phases(False)
            with dve.Else():
                all_phases(True)


_INS = ['x', 'src', 'dst', 'edge_attr_64', 'edge_weight', 'L0_gnn_We1', 'L0_gnn_be1', 'L0_gnn_We2', 'L0_gnn_be2',
        'L0_gnn_Wt', 'L0_gnn_bt', 'L0_gnn_Wn1', 'L0_gnn_bn1', 'L0_gnn_Wn2', 'L0_gnn_bn2', 'L1_gnn_W_rel0',
        'L1_gnn_b_rel0', 'L1_gnn_W_root0', 'L1_gnn_W_rel1', 'L1_gnn_b_rel1', 'L1_gnn_W_root1']
_OUT = ((6250, 128), 'float32')


def kernel(**inputs):
    import numpy as _np
    import concourse.bacc as _bacc
    from concourse import mybir as _mybir
    from concourse.bass_utils import run_bass_kernel_spmd as _run

    nc = _bacc.Bacc("TRN2", target_bir_lowering=False, num_devices=1)
    arrays, args = {}, []
    for name in _INS:
        a = _np.ascontiguousarray(inputs[name])
        arrays[f"in_{name}"] = a
        args.append(nc.dram_tensor(f"in_{name}", a.shape, _mybir.dt.from_np(a.dtype), kind="ExternalInput").ap())
    shape, dtype = _OUT
    args.append(nc.dram_tensor("out_0", shape, _mybir.dt.from_np(_np.dtype(dtype)), kind="ExternalOutput").ap())
    gnn_program(nc, *args)
    r = _run(nc, [arrays], core_ids=[0])
    return r.results[0]["out_0"]
```

```python
import concourse.bass as bass
from concourse import mybir
from contextlib import ExitStack


def gnn_program(nc, x, src, dst, edge_attr, edge_time, We1, be1, We2, be2, Wt, bt, Wn1, bn1, Wn2, bn2,
                Wr0, br0, Wo0, Wr1, br1, Wo1, out):
    f32, bf16, i32 = mybir.dt.float32, mybir.dt.bfloat16, mybir.dt.int32
    ALU, ACT, AX = mybir.AluOpType, mybir.ActivationFunctionType, mybir.AxisListType

    P = 128
    N, F = x.shape
    E, CH = edge_attr.shape
    NT = -(-N // P)
    NP = NT * P
    WN = P
    NWIN = NP // WN
    TPG = 4
    GE = TPG * P
    NG = -(-E // GE)
    LAST = E - GE
    REPEATED = NG * GE - E
    U = 4
    assert NG % U == 0 and F == P
    HALVES = 2
    CT = 7
    NCH = NT // CT
    CN = CT * P
    assert NCH * CT == NT and NCH == 7
    TAIL = N - (NT - 1) * P
    EPS = 1e-5
    NOWHERE = float(1 << 20)
    NPH = 3

    table = [nc.dram_tensor(f"table{i}", (NP, F), f32, kind="Internal").ap() for i in range(NPH)]

    ctx = ExitStack()
    with ctx:
        def sb(name, shape, dt=f32):
            return ctx.enter_context(nc.sbuf_tensor(name, shape, dt))

        def bank(name):
            return ctx.enter_context(nc.psum_tensor(name, [P, 512], f32))

        def sem(name):
            return ctx.enter_context(nc.semaphore(name))

        we1, we2 = sb("we1", [CH, P]), sb("we2", [P, P])
        wn1, wn2 = sb("wn1", [P, 2, P]), sb("wn2", [P, P])
        wr = [sb("wr0", [P, P]), sb("wr1", [P, P])]
        wo = [sb("wo0", [P, P]), sb("wo1", [P, P])]
        cols = sb("cols", [P, 4])
        be1_c, be2_c, wt_c, bt_c = (cols[:, i:i + 1] for i in range(4))
        bias_rows = sb("bias_rows", [P, NPH, P])
        bn2_row = sb("bn2_row", [1, P])
        ident = sb("ident", [P, P])
        iota = sb("iota", [P, WN])
        win_base = sb("win_base", [P, NWIN])
        ones = sb("ones", [P, P])
        ones16 = sb("ones16", [P, P], bf16)

        acc_a, acc_b, degree = sb("acc_a", [P, NP]), sb("acc_b", [P, NP]), sb("degree", [P, NP])
        acc = [acc_a, acc_b, acc_a]
        own = sb("own", [P, NT, F])

        GC = HALVES * P * TPG
        dst_abs, dst_rel, src_idx = sb("dst_abs", [P, GC]), sb("dst_rel", [P, GC]), sb("src_idx", [P, GC], i32)
        base_row = sb("base_row", [1, HALVES * P], i32)
        flag = sb("flag", [1, 1], i32)
        prep = own[:, 0:4 * HALVES * TPG, :].rearrange("p t f -> p (t f)").rearrange("p (a h e) -> p a h e", a=4, h=HALVES)
        dst_i, src_i = prep[:, 0].bitcast(i32), prep[:, 1].bitcast(i32)
        dst_g, src_g = prep[:, 2], prep[:, 3]
        lo, hi, base, over = (sb(n, [P, HALVES]) for n in ("lo", "hi", "base", "over"))
        over1, over_f = sb("over1", [P, 1]), sb("over_f", [1, 1])
        diag = sb("diag", [P, HALVES, P])

        ea = sb("ea", [P, U, TPG, CH])
        tsb = sb("tsb", [P, U, GE])
        eaT, h1, tw, efT = sb("eaT", [CH, 2, GE]), sb("h1", [P, 2, GE]), sb("tw", [P, 2, GE]), sb("efT", [P, 2, GE])
        idx = sb("idx", [P, U, TPG], i32)
        rows = sb("rows", [P, U, TPG, F])
        msg = sb("msg", [P, 2, TPG, F])
        onehot = sb("onehot", [P, 2, TPG, WN])
        rel_w = sb("rel_w", [P, TPG])

        xs, fm = sb("xs", [P, 2, CT, F]), sb("fm", [P, 2, CN])
        nm, done_rows = sb("nm", [P, 2, CT, F]), sb("done_rows", [P, 2, CT, F])
        deg_row = sb("deg_row", [1, 2, CN])
        stats, mv = sb("stats", [P, 2, CT, 6]), sb("mv", [P, 2, CT, 2])
        std, rstd, shift = (sb(n, [P, 2, CT]) for n in ("std", "rstd", "shift"))
        eps_c = sb("eps_c", [P, 1])

        B = [bank(f"bank{i}") for i in range(8)]
        ps_t, ps_h, ps_e, ps_z, ps_s, ps_d = B[:6]
        def pair(i):
            return [B[2 * i], B[2 * i + 1]]
        SPAN = [(0, 4), (4, CT)]

        def width(t):
            return (SPAN[t][1] - SPAN[t][0]) * P

        def in_fm(t):
            return slice(SPAN[t][0] * P, SPAN[t][1] * P)

        def as_rows(bank_ap, t):
            return bank_ap[:, 0:width(t)].rearrange("p (t f) -> p t f", f=F)

        s = {n: sem(n) for n in (
            "weights", "edges", "edge_pads", "first_weights", "consts", "ident_zero", "zeroed", "prep", "prep_pe", "masked", "lists_ready",
            "idx_ready", "t_done", "a_done", "m1_done", "h_done", "m2_done", "sig_done", "b_done", "m3_done",
            "c_done", "r_done", "oh_done", "seg_done", "acc_done", "gen_rel", "gen_oh", "gen_seg", "gen_acc",
            "link", "passed_SP", "passed_Pool", "passed_PE", "passed_DVE", "acc_a_clear", "own_part", "inverse")}
        ea_in = [sem(f"ea_in{u}") for u in range(U)]
        ts_in = [sem(f"ts_in{u}") for u in range(U)]
        gathered = [sem(f"gathered{u}") for u in range(U)]
        proj = [{n: sem(f"proj{m}_{n}") for n in ("in0", "in1", "turned", "fm", "product", "rows")} for m in range(NPH)]
        node = [{n: sem(f"node{m}_{n}") for n in (
            "in0", "in1", "lhs", "product", "added", "stats", "mv", "std", "rstd", "shift", "rows")} for m in range(NPH)]
        stored = [[sem(f"stored{m}_{u}") for u in range(2)] for m in range(NPH + 1)]

        def wait(eng, semaphore, value):
            if not isinstance(value, int) or value > 0:
                eng.wait_ge(semaphore, value)

        def wait_alone(eng, semaphore, value):
            wait(eng, semaphore, value)
            if not isinstance(value, int):
                eng.sem_inc(s["passed_" + str(eng.engine).split(".")[-1]], 1)

        def over_chunks(eng, step):
            for c in range(2):
                step(c, c, 0)
            with eng.Fori(1, NCH // 2) as i:
                for u in range(2):
                    step(2 * i + u, u, i)
            step(NCH - 1, (NCH - 1) % 2, (NCH - 1) // 2)

        def over_chunks_ahead(eng, step):
            for c in range(NCH):
                step(c, c % 2, c // 2)

        def in_use(u, i, lead):
            return i + (u + lead) // 2 + 1

        def is_chunk(c):
            return not isinstance(c, int) or c < NCH

        def over_steps(eng, step, lags):
            for k in range(2 * U):
                step(k, k % U, k)
            with eng.Fori(2, NG // U) as i:
                for u in range(U):
                    step(i * U + u, u, i)
            for k in range(NG, NG + lags):
                step(k, k % U, k)

        def has(k, lag):
            return not isinstance(k, int) or 0 <= k - lag < NG

        def table_stored(eng, m):
            eng.wait_ge(stored[m][0], 16 * (NCH // 2 + 1))
            eng.wait_ge(stored[m][1], 16 * (NCH // 2))

        block = ctx.enter_context(nc.Block())

        @block.sync
        def _(sp):
            cursor = [0]

            def one(dst_ap, src_ap, semaphore):
                sp.dma_start(dst_ap, src_ap).then_inc(semaphore, 16)

            def load_rows(semaphore, frm, c, u):
                if isinstance(c, int) and c == NCH - 1 and frm.shape[0] < NP:
                    sp.dma_start(xs[:, u, 0:CT - 1, :],
                                 frm[c * CN:c * CN + (CT - 1) * P, :].rearrange("(t p) f -> p t f", p=P)).then_inc(semaphore, 16)
                    sp.dma_start(xs[0:TAIL, u, CT - 1, :], frm[N - TAIL:N, :]).then_inc(semaphore, 16)
                else:
                    sp.dma_start(xs[:, u, :, :],
                                 frm[bass.ds(c * CN, CN), :].rearrange("(t p) f -> p t f", p=P)).then_inc(semaphore, 32)

            def store_rows(m, to, c, u):
                if isinstance(c, int) and c == NCH - 1 and to.shape[0] < NP:
                    sp.dma_start(to[c * CN:c * CN + (CT - 1) * P, :].rearrange("(t p) f -> p t f", p=P),
                                 done_rows[:, u, 0:CT - 1, :]).then_inc(stored[m][u], 16)
                    sp.dma_start(to[N - TAIL:N, :], done_rows[0:TAIL, u, CT - 1, :]).then_inc(stored[m][u], 16)
                else:
                    sp.dma_start(to[bass.ds(c * CN, CN), :].rearrange("(t p) f -> p t f", p=P),
                                 done_rows[:, u, :, :]).then_inc(stored[m][u], 16)

            for u in range(2):
                load_rows(proj[0][f"in{u}"], x, u, u)
            one(wn1[:, :, :], Wn1.rearrange("(a k) n -> k a n", a=2), s["first_weights"])
            one(bias_rows[:, 0, :], bn1.rearrange("(a n) -> a n", a=1).to_broadcast((P, P)), s["first_weights"])
            sp.wait_ge(s["edge_pads"], 2)
            full = (NG - 1 - P) // 64 * 64
            for to, frm in ((dst_i, dst), (src_i, src)):
                one(to[:, 0, :], frm[0:P * GE].rearrange("(q e) -> q e", e=GE), s["edges"])
                one(to[0:full, 1, :], frm[P * GE:(P + full) * GE].rearrange("(q e) -> q e", e=GE), s["edges"])
                one(to[full:NG - 1 - P, 1, :], frm[(P + full) * GE:(NG - 1) * GE].rearrange("(q e) -> q e", e=GE), s["edges"])
                one(to[NG - 1 - P:NG - P, 1, :], frm[LAST:E].rearrange("(q e) -> q e", e=GE), s["edges"])
            for w, d in ((we1, We1), (we2, We2), (wn2, Wn2), (wr[0], Wr0), (wr[1], Wr1), (wo[0], Wo0), (wo[1], Wo1)):
                one(w[:, :], d, s["weights"])
            for m, v in ((1, br0), (2, br1)):
                one(bias_rows[:, m, :], v.rearrange("(a n) -> a n", a=1).to_broadcast((P, P)), s["weights"])
            one(bn2_row[:, :], bn2.rearrange("(a n) -> a n", a=1), s["weights"])
            for i, v in enumerate((be1, be2, None, bt)):
                one(cols[:, i:i + 1], Wt.rearrange("a n -> n a") if v is None else v.rearrange("(n a) -> n a", a=1), s["weights"])

            def nodes0(c, u, i):
                wait(sp, proj[0]["rows"], c + 1)
                store_rows(0, table[0], c, u)
                if c + 2 < NCH:
                    load_rows(proj[0][f"in{u}"], x, c + 2, u)
            over_chunks_ahead(sp, nodes0)

            def edges(g, u, i):
                wait(sp, s["t_done"], g - U + 1)
                first = LAST if isinstance(g, int) and g == NG - 1 else g * GE
                sp.dma_start(ea[:, u, :, :], edge_attr[bass.ds(first, GE), :].rearrange("(p j) c -> p j c", j=TPG)).then_inc(ea_in[u], 16)
                wait_alone(sp, s["sig_done"], g - U + 1)
                sp.dma_start(tsb[:, u, :], edge_time[bass.ds(first, GE)].rearrange("(a e) -> a e", a=1).to_broadcast((P, GE))).then_inc(ts_in[u], 16)
            for g in range(U):
                edges(g, g, g)
            with sp.Fori(1, NG // U - 1) as i:
                for u in range(U):
                    edges(i * U + u, u, i)
            for g in range(NG - U, NG):
                edges(g, g % U, g)

            for u in range(2):
                load_rows(node[0][f"in{u}"], x, u, u)

            def nodes1(c, u, i):
                sp.wait_ge(node[0]["rows"], c + 1)
                store_rows(1, table[1], c, u)
                if c + 2 < NCH:
                    load_rows(node[0][f"in{u}"], x, c + 2, u)
            over_chunks_ahead(sp, nodes1)

            for m in (1, 2):
                table_stored(sp, m)

                def load_own(c, m=m):
                    wait(sp, proj[m]["rows"], c)
                    load_rows(proj[m]["in0"], table[m], c, 0)
                    if m == 2:
                        load_rows(proj[m]["in1"], table[1], c, 1)
                load_own(0)
                with sp.Fori(1, NCH) as c:
                    load_own(c)

                def store(c, u, i, m=m):
                    sp.wait_ge(node[m]["rows"], c + 1)
                    store_rows(m + 1, table[2] if m == 1 else out, c, u)
                over_chunks(sp, store)
            sp.wait_ge(stored[NPH][0], 16 * (NCH // 2 + 2))
            sp.wait_ge(stored[NPH][1], 16 * (NCH // 2))

        @block.gpsimd
        def _(pool):
            nc.gpsimd.memset(dst_i[:, 1, :], 0).then_inc(s["edge_pads"], 1)
            nc.gpsimd.memset(src_i[:, 1, :], 0).then_inc(s["edge_pads"], 1)
            nc.gpsimd.memset(ident[:, :], 0.0).then_inc(s["ident_zero"], 1)
            pool.wait_ge(s["ident_zero"], 1)
            nc.gpsimd.affine_select(out=ident[:, :], in_=ident[:, :], compare_op=ALU.not_equal, fill=1.0, base=0,
                                    pattern=[[-1, P]], channel_multiplier=1).then_inc(s["consts"], 1)
            nc.gpsimd.memset(ones[:, :], 1.0).then_inc(s["consts"], 1)
            nc.gpsimd.memset(ones16[:, :], 1.0).then_inc(s["consts"], 1)
            nc.gpsimd.iota(iota[:, :], pattern=[[1, WN]], base=0, channel_multiplier=0,
                           allow_small_or_imprecise_dtypes=True).then_inc(s["consts"], 1)
            nc.gpsimd.iota(win_base[:, :], pattern=[[WN, NWIN]], base=0, channel_multiplier=0,
                           allow_small_or_imprecise_dtypes=True).then_inc(s["consts"], 1)
            nc.gpsimd.memset(eps_c[:, :], EPS).then_inc(s["consts"], 1)
            for a in (acc_a, acc_b, degree):
                nc.gpsimd.memset(a[:, :], 0.0).then_inc(s["zeroed"], 1)
            pool.wait_ge(s["prep"], 1)
            q = NG - 1 - P
            nc.gpsimd.affine_select(out=dst_g[:, 1, :], in_=dst_g[:, 1, :], compare_op=ALU.is_ge, fill=NOWHERE,
                                    base=GE * 2 * q - REPEATED, pattern=[[1, GE]], channel_multiplier=-GE * 2).then_inc(s["masked"], 1)

            for ph in range(NPH):
                table_stored(pool, ph)

                def group(g, u, i, ph=ph):
                    pool.wait_ge(s["idx_ready"], ph * NG + g + 1)
                    if ph == 0:
                        wait_alone(pool, s["c_done"], g - U + 1)
                    elif not isinstance(g, int) or g >= U:
                        wait_alone(pool, s["seg_done"], ph * NG + g - U + 1)
                    for j in range(TPG):
                        nc.gpsimd.indirect_dma_start(
                            rows[:, u, j, :], None, table[ph][:, :],
                            bass.IndirectOffsetOnAxis(ap=idx[:, u, j:j + 1], axis=0)).then_inc(gathered[u], 16)
                for g in range(U):
                    group(g, g, 0)
                with pool.Fori(1, NG // U) as i:
                    for u in range(U):
                        group(i * U + u, u, i)

        @block.scalar
        def _(act):
            def stage_idx(ph, g, u, i):
                if not (isinstance(g, int) and g < U):
                    before = ph * (NG // U) + (g // U if isinstance(g, int) else i)
                    act.wait_ge(gathered[u], 16 * TPG * before)
                nc.scalar.copy(idx[:, u, :], src_idx[:, bass.ds(g * TPG, TPG)]).then_inc(s["idx_ready"], 1)

            def turn(m, c, u):
                act.wait_ge(proj[m]["turned"], c + 1)
                wait(act, proj[m]["product"], c - 1 if m == 0 else c)
                for t in range(2):
                    last = nc.scalar.copy(fm[:, u, in_fm(t)], pair(0)[t][:, 0:width(t)])
                last.then_inc(proj[m]["fm"], 1)

            over_chunks(act, lambda c, u, i: turn(0, c, u))
            act.wait_ge(s["weights"], 16 * 14)
            act.wait_ge(s["lists_ready"], 1)

            def step(k, u, i):
                if has(k, 0):
                    stage_idx(0, k, u, i)
                if has(k, 1):
                    g = k - 1
                    act.wait_ge(s["m1_done"], g + 1)
                    wait(act, s["m2_done"], g - 1)
                    nc.scalar.activation(h1[:, (u - 1) % 2, :], ps_h[:, :], ACT.Relu, bias=be1_c).then_inc(s["h_done"], 1)
                if has(k, 2):
                    g = k - 2
                    v = (u - 2) % U
                    use = g // U + 1 if isinstance(g, int) else (i + 1 if u >= 2 else i)
                    act.wait_ge(ts_in[v], 16 * use)
                    wait(act, s["b_done"], g - 1)
                    nc.scalar.activation(tw[:, v % 2, :].rearrange("f (j p) -> f j p", j=TPG),
                                         tsb[:, v, :].rearrange("f (p j) -> f j p", j=TPG),
                                         ACT.Sigmoid, scale=wt_c, bias=bt_c).then_inc(s["sig_done"], 1)
                if has(k, 3):
                    g = k - 3
                    act.wait_ge(s["c_done"], g + 1)
                    m = msg[:, (u - 3) % 2, :, :]
                    nc.scalar.activation(m, m, ACT.Relu).then_inc(s["r_done"], 1)
            over_steps(act, step, 5)

            def deviations(n, c, v):
                act.wait_ge(node[n]["mv"], c + 1)
                nc.scalar.activation(std[:, v, :], mv[:, v, :, 1], ACT.Sqrt, bias=eps_c[:, :]).then_inc(node[n]["std"], 1)

            def norm(n, c, u, i):
                act.wait_ge(node[n]["shift"], c + 1)
                wait(act, stored[n + 1][u], 16 * i)
                for j in range(CT):
                    last = nc.scalar.activation(done_rows[:, u, j, :], nm[:, u, j, :], ACT.Identity,
                                                scale=rstd[:, u, j:j + 1], bias=shift[:, u, j:j + 1])
                last.then_inc(node[n]["rows"], 1)
                if is_chunk(c + 1):
                    deviations(n, c + 1, (u + 1) % 2)

            def stationary(c, u):
                wait(act, node[0]["product"], c - 1)
                nc.scalar.copy(deg_row[:, u, :], degree[0:1, bass.ds(c * CN, CN)])
                nc.scalar.copy(fm[:, u, :], acc_a[:, bass.ds(c * CN, CN)]).then_inc(node[0]["lhs"], 1)

            def nodes1(c, u, i):
                if is_chunk(c + 2):
                    stationary(c + 2, u)
                norm(0, c, u, i)
            act.wait_ge(s["acc_done"], NG)
            table_stored(act, 0)
            stationary(0, 0)
            stationary(1, 1)
            deviations(0, 0, 0)
            over_chunks_ahead(act, nodes1)

            for ph in (1, 2):
                for g in range(U):
                    act.wait_ge(gathered[g], 16 * TPG * ph * (NG // U))
                    nc.scalar.copy(idx[:, g, :], src_idx[:, g * TPG:(g + 1) * TPG]).then_inc(s["idx_ready"], 1)
                for g in range(U, 2 * U):
                    stage_idx(ph, g, g - U, 1)
                def round_(i):
                    for u in range(U):
                        stage_idx(ph, (i + 1) * U + u, u, i + 1)
                    turn(ph, i - 1, 0)
                round_(1)
                with act.Fori(2, NCH + 1) as i:
                    round_(i)
                with act.Fori(NCH + 2, NG // U) as i:
                    for u in range(U):
                        stage_idx(ph, i * U + u, u, i)

                def relu(c, u, i):
                    act.wait_ge(node[1]["added"], c + 1)
                    wait(act, stored[2][u], 16 * i)
                    nc.scalar.activation(done_rows[:, u, :, :], nm[:, u, :, :], ACT.Relu).then_inc(node[1]["rows"], 1)
                table_stored(act, ph)
                if ph == 1:
                    over_chunks(act, relu)
                else:
                    deviations(2, 0, 0)
                    over_chunks(act, lambda c, u, i: norm(2, c, u, i))

        @block.tensor
        def _(pe):
            def transposes(dst_banks, src_of):
                for t in range(2):
                    for j in range(*SPAN[t]):
                        o = (j - SPAN[t][0]) * P
                        last = nc.tensor.transpose(dst_banks[t][:, o:o + P], src_of(j), ident[:, :])
                return last

            pe.wait_ge(s["consts"], 6)
            pe.wait_ge(s["first_weights"], 32)

            def turn(m, c, u, use):
                pe.wait_ge(proj[m]["in0" if m else f"in{u}"], 32 * use)
                wait(pe, proj[m]["fm"], c)
                transposes(pair(0), lambda j: xs[:, u, j, :]).then_inc(proj[m]["turned"], 1)

            def product(m, c, u, w):
                pe.wait_ge(proj[m]["fm"], c + 1)
                wait(pe, proj[m]["rows"], c)
                for t in range(2):
                    for j in range(*SPAN[t]):
                        o = (j - SPAN[t][0]) * P
                        last = nc.tensor.matmul(pair(1)[t][:, o:o + P], fm[:, u, j * P:(j + 1) * P], w, start=True, stop=True)
                last.then_inc(proj[m]["product"], 1)

            def nodes0(c, u, i):
                if is_chunk(c + 1):
                    turn(0, c + 1, (u + 1) % 2, in_use(u, i, 1))
                product(0, c, u, wn1[:, 0, :])
            turn(0, 0, 0, 1)
            over_chunks(pe, nodes0)

            pe.wait_ge(s["prep"], 2)
            nc.tensor.transpose(B[6][0:1, 0:P], over1[:, :], ident[:, :])
            for h in range(HALVES):
                nc.tensor.transpose(B[6][0:1, (h + 1) * P:(h + 2) * P], base[:, h:h + 1], ident[:, :])
            for h in range(HALVES):
                last = nc.tensor.matmul(B[7][:, h * P:(h + 1) * P], ones[:, :], diag[:, h, :], start=True, stop=True)
            pe.wait_ge(s["masked"], 1)
            pe.wait_ge(proj[0]["rows"], NCH)
            for n, lists in enumerate((dst_g, src_g)):
                for h in range(HALVES):
                    for j in range(TPG):
                        v = lists[:, h, :].rearrange("q (p j) -> q j p", j=TPG)[:, j, :]
                        last = nc.tensor.transpose(B[2 * n + h][:, j * P:(j + 1) * P], v, ident[:, :])
            last.then_inc(s["prep_pe"], 1)
            pe.wait_ge(s["weights"], 16 * 14)
            pe.wait_ge(s["lists_ready"], 1)

            def segment_sum(ph, k, lag, u, i, general):
                g = k - lag
                v = (u - lag) % U
                seq = ph * NG + g
                if ph == 0:
                    wait_alone(pe, s["r_done"], g + 1)
                    data = msg[:, v % 2, :, :]
                else:
                    use = ph * (NG // U) + (g // U + 1 if isinstance(g, int) else (i + 1))
                    wait_alone(pe, gathered[v], 16 * TPG * use)
                    data = rows[:, v, :, :]

                def window(oh, signal):
                    for j in range(TPG):
                        last = nc.tensor.matmul(ps_s[:, 0:WN], data[:, j, :], oh[:, j, :], start=(j == 0), stop=(j == TPG - 1))
                        if ph == 0:
                            half = oh[:, j, :].bitcast(bf16).rearrange("p (n t) -> p t n", t=2)[:, 1, :]
                            last = nc.tensor.matmul(ps_d[:, 0:WN], ones16[:, :], half, start=(j == 0), stop=(j == TPG - 1))
                    last.then_inc(signal, 1)
                if general:
                    oh = onehot[:, 0, :, :]
                    with pe.Fori(0, NWIN - 1) as w:
                        pe.wait_ge(s["gen_oh"], seq * NWIN + w + 1)
                        window(oh, s["gen_seg"])
                    pe.wait_ge(s["gen_oh"], seq * NWIN + NWIN)
                    window(oh, s["seg_done"])
                else:
                    pe.wait_ge(s["oh_done"], seq + 1)
                    wait(pe, s["acc_done"], seq)
                    window(onehot[:, v % 2, :, :], s["seg_done"])

            def step_of(general):
                def step(k, u, i):
                    if has(k, 0):
                        use = k // U + 1 if isinstance(k, int) else i + 1
                        pe.wait_ge(ea_in[u], 16 * use)
                        wait_alone(pe, s["a_done"], k)
                        for j in range(TPG):
                            last = nc.tensor.transpose(ps_t[0:CH, j * P:(j + 1) * P], ea[:, u, j, :], ident[:, :])
                        last.then_inc(s["t_done"], 1)
                    if has(k, 1):
                        g = k - 1
                        pe.wait_ge(s["a_done"], g + 1)
                        wait(pe, s["h_done"], g)
                        nc.tensor.matmul(ps_h[:, :], we1[:, :], eaT[:, (u - 1) % 2, :], start=True, stop=True).then_inc(s["m1_done"], 1)
                    if has(k, 2):
                        g = k - 2
                        pe.wait_ge(s["h_done"], g + 1)
                        wait(pe, s["b_done"], g)
                        nc.tensor.matmul(ps_e[:, :], we2[:, :], h1[:, (u - 2) % 2, :], start=True, stop=True).then_inc(s["m2_done"], 1)
                    if has(k, 3):
                        g = k - 3
                        pe.wait_ge(s["b_done"], g + 1)
                        wait(pe, s["c_done"], g)
                        for j in range(TPG):
                            last = nc.tensor.matmul(ps_z[:, j * P:(j + 1) * P], efT[:, (u - 3) % 2, j * P:(j + 1) * P],
                                                    wn1[:, 1, :], start=True, stop=True)
                        last.then_inc(s["m3_done"], 1)
                    if has(k, 4):
                        segment_sum(0, k, 4, u, i, general)
                return step

            def node_products(n):
                def chunk(c, u, i):
                    pe.wait_ge(node[n]["lhs"], c + 1)
                    wait(pe, node[n]["added"], c - 1)
                    for t in range(2):
                        for j in range(*SPAN[t]):
                            o = (j - SPAN[t][0]) * P
                            at = pair(u)[t][:, o:o + P]
                            last = nc.tensor.matmul(at, fm[:, u, j * P:(j + 1) * P], wn2[:, :] if n == 0 else wr[n - 1][:, :],
                                                    start=True, stop=(n > 0))
                            if n == 0:
                                last = nc.tensor.matmul(at, deg_row[:, u, j * P:(j + 1) * P], bn2_row[:, :], start=False, stop=True)
                    last.then_inc(node[n]["product"], 1)
                return chunk

            def all_phases(general):
                over_steps(pe, step_of(general), 5)
                over_chunks(pe, node_products(0))
                for ph in (1, 2):
                    pe.wait_ge(node[ph - 1]["added"], NCH)
                    for g in range(U):
                        segment_sum(ph, g, 0, g, 0, general)
                    def round_(i, ph=ph):
                        for u in range(U):
                            segment_sum(ph, i * U + u, 0, u, i, general)
                        turn(ph, i - 1, 0, i)
                        product(ph, i - 1, 0, wo[ph - 1][:, :])
                    round_(1)
                    with pe.Fori(2, NCH + 1) as i:
                        round_(i)
                    with pe.Fori(NCH + 1, NG // U) as i:
                        for u in range(U):
                            segment_sum(ph, i * U + u, 0, u, i, general)
                    pe.wait_ge(proj[ph]["rows"], NCH)
                    over_chunks(pe, node_products(ph))

            spread = pe.value_load(flag[0:1, 0:1], min_val=0, max_val=1)
            with pe.If(spread == 0):
                all_phases(False)
            with pe.Else():
                all_phases(True)

        @block.vector
        def _(dve):
            steps = [0]

            def link(ins):
                steps[0] += 1
                ins.then_inc(s["link"], 1)
                dve.wait_ge(s["link"], steps[0])

            def project(m, c, u, before):
                dve.wait_ge(proj[m]["product"], c + 1)
                if m == 0:
                    wait(dve, stored[0][u], 16 * before)
                for t in range(2):
                    a, b = SPAN[t]
                    to = done_rows[:, u, a:b, :] if m == 0 else own[:, bass.ds(c * CT + a, b - a), :] if m == 1 else nm[:, 0, a:b, :]
                    last = nc.vector.tensor_tensor(to, as_rows(pair(1)[t], t),
                                                   bias_rows[:, m:m + 1, :].to_broadcast((P, b - a, F)), ALU.add)
                if m == 2:
                    last.then_inc(s["own_part"], 1)
                    dve.wait_ge(s["own_part"], c + 1)
                    dve.wait_ge(proj[2]["in1"], 32 * (c + 1))
                    last = nc.vector.tensor_tensor(own[:, bass.ds(c * CT, CT), :], nm[:, 0, :, :], xs[:, 1, :, :], ALU.add)
                last.then_inc(proj[m]["rows"], 1)

            dve.wait_ge(s["edges"], 16 * 8)
            link(nc.vector.tensor_copy(dst_g[:, :, :], dst_i[:, :, :]))
            nc.vector.tensor_copy(src_g[:, :, :], src_i[:, :, :])
            nc.vector.tensor_reduce(lo[:, :], dst_g[:, :, :], AX.X, ALU.min)
            nc.vector.tensor_reduce(hi[:, :], dst_g[:, :, :], AX.X, ALU.max).then_inc(s["prep"], 1)
            dve.wait_ge(s["prep"], 1)
            link(nc.vector.tensor_scalar(base[:, :], lo[:, :], float(NP - WN), None, ALU.min))
            link(nc.vector.tensor_tensor(over[:, :], hi[:, :], base[:, :], ALU.subtract))
            link(nc.vector.tensor_reduce(over1[:, :], over[:, :], AX.X, ALU.max))
            dve.wait_ge(s["consts"], 6)
            for h in range(HALVES):
                last = nc.vector.tensor_scalar(diag[:, h, :], ident[:, :], base[:, h:h + 1], None, ALU.mult)
            last.then_inc(s["prep"], 1)

            dve.wait_ge(s["first_weights"], 32)
            over_chunks(dve, lambda c, u, i: project(0, c, u, i))

            dve.wait_ge(s["prep_pe"], 1)
            link(nc.vector.tensor_reduce(over_f[:, :], B[6][0:1, 0:P], AX.X, ALU.max))
            nc.vector.tensor_scalar(flag[:, :], over_f[:, :], float(WN), None, ALU.is_ge)
            nc.vector.tensor_copy(base_row[:, :], B[6][0:1, P:(1 + HALVES) * P])
            for h in range(HALVES):
                to = dst_abs[:, h * P * TPG:(h + 1) * P * TPG].rearrange("p (q j) -> p q j", j=TPG)
                nc.vector.tensor_copy(to, B[h][:, :].rearrange("p (j q) -> p q j", j=TPG))
                to = src_idx[:, h * P * TPG:(h + 1) * P * TPG].rearrange("p (q j) -> p q j", j=TPG)
                last = nc.vector.tensor_copy(to, B[2 + h][:, :].rearrange("p (j q) -> p q j", j=TPG))
            link(last)
            for h in range(HALVES):
                to, frm = (a[:, h * P * TPG:(h + 1) * P * TPG].rearrange("p (q j) -> p q j", j=TPG) for a in (dst_rel, dst_abs))
                for j in range(TPG):
                    last = nc.vector.tensor_tensor(to[:, :, j], frm[:, :, j], B[7][:, h * P:(h + 1) * P], ALU.subtract)
            last.then_inc(s["lists_ready"], 1)
            dve.wait_ge(s["lists_ready"], 1)
            dve.wait_ge(s["weights"], 16 * 14)

            dve.wait_ge(s["zeroed"], 3)

            def one_hots(seq, cols_ap, v, signal):
                for j in range(TPG):
                    last = nc.vector.tensor_scalar(onehot[:, v, j, :], iota[:, :], cols_ap(j), None, ALU.is_equal)
                last.then_inc(signal, 1)

            def fast_one_hots(ph, g, v):
                wait(dve, s["seg_done"], ph * NG + g - 1)
                one_hots(None, lambda j: dst_rel[:, bass.ds(g * TPG + j, 1)], v % 2, s["oh_done"])

            def fast_add(ph, g, at):
                seq = ph * NG + g
                dve.wait_ge(s["seg_done"], seq + 1)
                wait(dve, s["acc_done"], seq)
                if ph == 0:
                    o = degree[:, bass.ds(at, WN)]
                    nc.vector.tensor_tensor(o, o, ps_d[:, 0:WN], ALU.add)
                o = acc[ph][:, bass.ds(at, WN)]
                nc.vector.tensor_tensor(o, o, ps_s[:, 0:WN], ALU.add).then_inc(s["acc_done"], 1)

            def base_of(g):
                return dve.value_load(base_row[0:1, bass.ds(g, 1)], min_val=0, max_val=NP - WN)

            def all_windows(ph, g):
                seq = ph * NG + g

                def window(w, at, signal, value):
                    nc.vector.tensor_scalar(rel_w[:, :], dst_abs[:, bass.ds(g * TPG, TPG)], win_base[:, bass.ds(w, 1)], None,
                                            ALU.subtract).then_inc(s["gen_rel"], 1)
                    dve.wait_ge(s["gen_rel"], seq * NWIN + w + 1)
                    one_hots(None, lambda j: rel_w[:, j:j + 1], 0, s["gen_oh"])
                    dve.wait_ge(signal, value)
                    if ph == 0:
                        o = degree[:, bass.ds(at, WN)]
                        nc.vector.tensor_tensor(o, o, ps_d[:, 0:WN], ALU.add)
                    o = acc[ph][:, bass.ds(at, WN)]
                    nc.vector.tensor_tensor(o, o, ps_s[:, 0:WN], ALU.add).then_inc(s["gen_acc"], 1)
                    dve.wait_ge(s["gen_acc"], seq * NWIN + w + 1)
                with dve.Fori(0, NWIN - 1) as w:
                    window(w, w * WN, s["gen_seg"], seq * (NWIN - 1) + w + 1)
                window(NWIN - 1, (NWIN - 1) * WN, s["seg_done"], seq + 1)
                dve.sem_inc(s["acc_done"], 1)

            def step_of(general):
                def step(k, u, i):
                    if has(k, 0):
                        dve.wait_ge(s["t_done"], k + 1)
                        wait(dve, s["m1_done"], k - 1)
                        nc.vector.tensor_copy(eaT[:, u % 2, :], ps_t[0:CH, :]).then_inc(s["a_done"], 1)
                    if not general and has(k, 5):
                        fast_add(0, k - 5, base_of(k - 5))
                    if not general and has(k, 3):
                        fast_one_hots(0, k - 3, u - 3)
                    if has(k, 2):
                        g = k - 2
                        dve.wait_ge(s["m2_done"], g + 1)
                        dve.wait_ge(s["sig_done"], g + 1)
                        wait(dve, s["m3_done"], g - 1)
                        nc.vector.scalar_tensor_tensor(out=efT[:, u % 2, :], in0=ps_e[:, :], scalar=be2_c, in1=tw[:, u % 2, :],
                                                       op0=ALU.add, op1=ALU.mult).then_inc(s["b_done"], 1)
                    if has(k, 3):
                        g = k - 3
                        v = (u - 3) % U
                        use = g // U + 1 if isinstance(g, int) else (i + 1 if u == 3 else i)
                        dve.wait_ge(s["m3_done"], g + 1)
                        dve.wait_ge(gathered[v], 16 * TPG * use)
                        wait(dve, s["seg_done"], g - 1)
                        nc.vector.tensor_tensor(msg[:, v % 2, :, :], ps_z[:, :].rearrange("p (j f) -> p j f", j=TPG),
                                                rows[:, v, :, :], ALU.add).then_inc(s["c_done"], 1)
                    if general and has(k, 4):
                        all_windows(0, k - 4)
                return step

            def norm_scale(n, c, u):
                dve.wait_ge(node[n]["std"], c + 1)
                nc.vector.reciprocal(rstd[:, u, :], std[:, u, :]).then_inc(node[n]["rstd"], 1)
                dve.wait_ge(node[n]["rstd"], c + 1)
                nc.vector.scalar_tensor_tensor(out=shift[:, u, :], in0=mv[:, u, :, 0], scalar=-1.0, in1=rstd[:, u, :],
                                               op0=ALU.mult, op1=ALU.mult).then_inc(node[n]["shift"], 1)

            def moments(n, c, v):
                dve.wait_ge(node[n]["added"], c + 1)
                for j in range(CT):
                    last = nc.vector.bn_stats(stats[:, v, j, :], nm[:, v, j, :])
                last.then_inc(node[n]["stats"], 1)
                wait_alone(dve, node[n]["stats"], c + 1)
                for j in range(CT):
                    last = nc.vector.bn_aggr(mv[:, v, j, :], stats[:, v, j, :])
                last.then_inc(node[n]["mv"], 1)

            def messages_and_x(c, v, use):
                dve.wait_ge(node[0]["product"], c + 1)
                dve.wait_ge(node[0][f"in{v}"], 32 * use)
                for t in range(2):
                    a, b = SPAN[t]
                    last = nc.vector.scalar_tensor_tensor(out=nm[:, v, a:b, :], in0=xs[:, v, a:b, :], scalar=2.0,
                                                          in1=as_rows(pair(v)[t], t), op0=ALU.mult, op1=ALU.add)
                last.then_inc(node[0]["added"], 1)
                moments(0, c, v)

            def nodes1(c, u, i):
                norm_scale(0, c, u)
                if is_chunk(c + 1):
                    messages_and_x(c + 1, (u + 1) % 2, in_use(u, i, 1))

            def means(n, c, u):
                wait(dve, node[n]["product"], c - 1)
                nc.vector.tensor_tensor(fm[:, u, :], acc[n][:, bass.ds(c * CN, CN)], degree[:, bass.ds(c * CN, CN)],
                                        ALU.mult).then_inc(node[n]["lhs"], 1)

            def add_own(n, c, v):
                dve.wait_ge(node[n]["product"], c + 1)
                if n == 1:
                    wait(dve, node[1]["rows"], c)
                for t in range(2):
                    a, b = SPAN[t]
                    last = nc.vector.tensor_tensor(nm[:, v, a:b, :], as_rows(pair(v)[t], t),
                                                   own[:, bass.ds(c * CT + a, b - a), :], ALU.add)
                last.then_inc(node[n]["added"], 1)

            def nodes2(c, u, i):
                if is_chunk(c + 1):
                    means(1, c + 1, (u + 1) % 2)
                add_own(1, c, u)

            def nodes3(c, u, i):
                if is_chunk(c + 2):
                    means(2, c + 2, u)
                norm_scale(2, c, u)
                if is_chunk(c + 1):
                    add_own(2, c + 1, (u + 1) % 2)
                    moments(2, c + 1, (u + 1) % 2)

            def inverse_degree(c):
                at = degree[:, bass.ds(c * CN, CN)]
                nc.vector.tensor_scalar(at, at, 1.0, None, ALU.max).then_inc(s["inverse"], 1)
                wait_alone(dve, s["inverse"], 2 * c + 1)
                nc.vector.reciprocal(at, at).then_inc(s["inverse"], 1)

            def all_phases(general):
                over_steps(dve, step_of(general), 6)
                dve.wait_ge(s["acc_done"], NG)
                messages_and_x(0, 0, 1)
                over_chunks(dve, nodes1)
                for ph in (1, 2):
                    def groups(first, i, ph=ph):
                        for u in range(U):
                            g = i * U + u
                            if general:
                                all_windows(ph, g)
                                continue
                            fast_one_hots(ph, g, u)
                            if not (first and u == 0):
                                fast_add(ph, g - 1, base_of(g - 1))
                    groups(True, 0)
                    if ph == 1:
                        dve.wait_ge(node[0]["lhs"], NCH)
                        nc.vector.memset(acc_a[:, :], 0.0).then_inc(s["acc_a_clear"], 1)
                        dve.wait_ge(s["acc_a_clear"], 1)
                    with dve.Fori(1, NCH + 1) as i:
                        groups(False, i)
                        if ph == 1:
                            inverse_degree(i - 1)
                        project(ph, i - 1, 0, None)
                    with dve.Fori(NCH + 1, NG // U) as i:
                        groups(False, i)
                    if not general:
                        fast_add(ph, NG - 1, base_of(NG - 1))
                    dve.wait_ge(s["acc_done"], (ph + 1) * NG)
                    dve.wait_ge(proj[ph]["rows"], NCH)
                    means(ph, 0, 0)
                    if ph == 1:
                        over_chunks(dve, nodes2)
                    else:
                        means(2, 1, 1)
                        add_own(2, 0, 0)
                        moments(2, 0, 0)
                        over_chunks_ahead(dve, nodes3)

            spread = dve.value_load(flag[0:1, 0:1], min_val=0, max_val=1)
            with dve.If(spread == 0):
                all_phases(False)
            with dve.Else():
                all_phases(True)


_INS = ['x', 'src', 'dst', 'edge_attr_64', 'edge_weight', 'L0_gnn_We1', 'L0_gnn_be1', 'L0_gnn_We2', 'L0_gnn_be2',
        'L0_gnn_Wt', 'L0_gnn_bt', 'L0_gnn_Wn1', 'L0_gnn_bn1', 'L0_gnn_Wn2', 'L0_gnn_bn2', 'L1_gnn_W_rel0',
        'L1_gnn_b_rel0', 'L1_gnn_W_root0', 'L1_gnn_W_rel1', 'L1_gnn_b_rel1', 'L1_gnn_W_root1']
_OUT = ((6250, 128), 'float32')


def kernel(**inputs):
    import numpy as _np
    import concourse.bacc as _bacc
    from concourse import mybir as _mybir
    from concourse.bass_utils import run_bass_kernel_spmd as _run

    nc = _bacc.Bacc("TRN2", target_bir_lowering=False, num_devices=1)
    arrays, args = {}, []
    for name in _INS:
        a = _np.ascontiguousarray(inputs[name])
        arrays[f"in_{name}"] = a
        args.append(nc.dram_tensor(f"in_{name}", a.shape, _mybir.dt.from_np(a.dtype), kind="ExternalInput").ap())
    shape, dtype = _OUT
    args.append(nc.dram_tensor("out_0", shape, _mybir.dt.from_np(_np.dtype(dtype)), kind="ExternalOutput").ap())
    gnn_program(nc, *args)
    r = _run(nc, [arrays], core_ids=[0])
    return r.results[0]["out_0"]
```

```python
import concourse.bass as bass
from concourse import mybir
from contextlib import ExitStack


def gnn_program(nc, x, src, dst, edge_attr, edge_time, We1, be1, We2, be2, Wt, bt, Wn1, bn1, Wn2, bn2,
                Wr0, br0, Wo0, Wr1, br1, Wo1, out):
    f32, bf16, i32 = mybir.dt.float32, mybir.dt.bfloat16, mybir.dt.int32
    ALU, ACT, AX = mybir.AluOpType, mybir.ActivationFunctionType, mybir.AxisListType

    P = 128
    N, F = x.shape
    E, CH = edge_attr.shape
    NT = -(-N // P)
    NP = NT * P
    WN = P
    NWIN = NP // WN
    TPG = 4
    GE = TPG * P
    NG = -(-E // GE)
    LAST = E - GE
    REPEATED = NG * GE - E
    U = 4
    assert NG % U == 0 and F == P
    HALVES = 2
    CT = 7
    NCH = NT // CT
    CN = CT * P
    BR = 4
    NODE_ROUND = NG // U - 2 - (NCH - 2) * BR
    LAG = 5
    LAST_DUE = NG - 3
    assert 2 * CH == P and NCH * CT == NT and NCH == 7 and NODE_ROUND > 2 * NCH + 1
    TAIL = N - (NT - 1) * P
    EPS = 1e-5
    NOWHERE = float(1 << 20)
    NPH = 3

    table = [nc.dram_tensor(f"table{i}", (NP, F), f32, kind="Internal").ap() for i in range(NPH)]

    ctx = ExitStack()
    with ctx:
        def sb(name, shape, dt=f32):
            return ctx.enter_context(nc.sbuf_tensor(name, shape, dt))

        def bank(name):
            return ctx.enter_context(nc.psum_tensor(name, [P, 512], f32))

        def sem(name):
            return ctx.enter_context(nc.semaphore(name))

        we1, we2 = sb("we1", [P, 2, P]), sb("we2", [P, P])
        wn1, wn2 = sb("wn1", [P, 2, P]), sb("wn2", [P, P])
        wr = [sb("wr0", [P, P]), sb("wr1", [P, P])]
        wo = [sb("wo0", [P, P]), sb("wo1", [P, P])]
        cols = sb("cols", [P, 4])
        be1_c, be2_c, wt_c, bt_c = (cols[:, i:i + 1] for i in range(4))
        bias_rows = sb("bias_rows", [P, NPH, P])
        bn2_row = sb("bn2_row", [1, P])
        ident = sb("ident", [P, P])
        iota = sb("iota", [P, WN])
        win_base = sb("win_base", [P, NWIN])
        ones = sb("ones", [P, P])
        ones16 = sb("ones16", [P, P], bf16)

        acc_a, acc_b, degree = sb("acc_a", [P, NP]), sb("acc_b", [P, NP]), sb("degree", [P, NP])
        acc = [acc_a, acc_b, acc_a]
        x_rows = acc_b[:, :].rearrange("p (t f) -> p t f", f=F)
        own = sb("own", [P, NT, F])

        GC = HALVES * P * TPG
        dst_abs, dst_rel, src_idx = sb("dst_abs", [P, GC]), sb("dst_rel", [P, GC]), sb("src_idx", [P, GC], i32)
        base_row = sb("base_row", [1, HALVES * P], i32)
        flag = sb("flag", [1, 1], i32)
        prep = own[:, 0:4 * HALVES * TPG, :].rearrange("p t f -> p (t f)").rearrange("p (a h e) -> p a h e", a=4, h=HALVES)
        dst_i, src_i = prep[:, 0].bitcast(i32), prep[:, 1].bitcast(i32)
        dst_g, src_g = prep[:, 2], prep[:, 3]
        lo, hi, base, over = (sb(n, [P, HALVES]) for n in ("lo", "hi", "base", "over"))
        over1, over_f = sb("over1", [P, 1]), sb("over_f", [1, 1])
        past_due = sb("past_due", [P, HALVES, NCH])
        due, late = sb("due", [P, HALVES]), sb("late", [P, HALVES])
        diag = sb("diag", [P, HALVES, P])

        ea = sb("ea", [P, U, TPG, CH])
        tsb = sb("tsb", [P, U, GE])
        eaT, h1, tw, efT = sb("eaT", [2 * CH, 2, GE // 2]), sb("h1", [P, 2, GE]), sb("tw", [P, 2, GE]), sb("efT", [P, 2, GE])
        idx = sb("idx", [P, U, TPG], i32)
        rows = sb("rows", [P, U, TPG, F])
        msg = sb("msg", [P, 2, TPG, F])
        onehot = sb("onehot", [P, 2, TPG, WN])
        rel_w = sb("rel_w", [P, TPG])

        xs, fm = sb("xs", [P, 2, CT, F]), sb("fm", [P, 2, CN])
        nm, done_rows = sb("nm", [P, 2, CT, F]), sb("done_rows", [P, 2, CT, F])
        stats, mv = sb("stats", [P, 2, CT, 6]), sb("mv", [P, 2, CT, 2])
        std, rstd, shift = (sb(n, [P, 2, CT]) for n in ("std", "rstd", "shift"))
        eps_c = sb("eps_c", [P, 1])

        B = [bank(f"bank{i}") for i in range(8)]
        ps_t, ps_h, ps_e, ps_z, ps_s, ps_d = B[:6]
        def pair(i):
            return [B[2 * i], B[2 * i + 1]]
        def turned_in(u):
            return pair(0) if u == 0 else pair(3)
        SPAN = [(0, 4), (4, CT)]

        BOTH = (0, 1)

        def tiles_of(ts):
            a, b = SPAN[ts[0]][0], SPAN[ts[-1]][1]
            return a, a + round((b - a) * 4 / 7), b

        def width(t):
            return (SPAN[t][1] - SPAN[t][0]) * P

        def in_fm(t):
            return slice(SPAN[t][0] * P, SPAN[t][1] * P)

        def as_rows(bank_ap, t):
            return bank_ap[:, 0:width(t)].rearrange("p (t f) -> p t f", f=F)

        s = {n: sem(n) for n in (
            "ident_zero", "consts", "edge_pads", "zeroed", "first_weights", "weights", "src_in", "dst_in", "src_cast",
            "src_turned", "src_ready", "prep", "masked", "dst_turned", "bounds", "lists_ready", "link",
            "idx_ready", "attrs_turned", "attrs_copied", "hidden_product", "hidden_ready", "features_product", "time_weights",
            "features_ready", "message_product", "message_summed", "message_ready", "onehots_ready", "window_summed",
            "window_added",
            "any_relative", "any_onehots", "any_summed", "any_added",
            "acc_clear", "own_part", "inverse", "passed_SP", "passed_Pool", "passed_PE", "passed_DVE")}
        ea_in = [sem(f"ea_in{u}") for u in range(U)]
        ts_in = [sem(f"ts_in{u}") for u in range(U)]
        gathered = [sem(f"gathered{u}") for u in range(U)]
        proj = [{n: sem(f"proj{m}_{n}") for n in ("loaded", "x1_loaded", "turned", "fm", "product", "bank", "rows")} for m in range(NPH)]
        node = [{n: sem(f"node{m}_{n}") for n in (
            "lhs", "product", "added", "stats", "mv", "std", "rstd", "shift", "rows", "rows_v")} for m in range(NPH)]
        x_in = [sem(f"x_in{c}") for c in range(NCH)]
        tables = sem("tables")
        stored = [[sem(f"stored{m}_{u}") for u in range(2)] for m in range(NPH + 1)]

        def wait(eng, semaphore, value):
            if not isinstance(value, int) or value > 0:
                eng.wait_ge(semaphore, value)

        def wait_alone(eng, semaphore, value):
            wait(eng, semaphore, value)
            if not isinstance(value, int):
                eng.sem_inc(s["passed_" + str(eng.engine).split(".")[-1]], 1)

        def over_chunks(eng, step):
            for c in range(2):
                step(c, c, 0)
            with eng.Fori(1, NCH // 2) as i:
                for u in range(2):
                    step(2 * i + u, u, i)
            step(NCH - 1, (NCH - 1) % 2, (NCH - 1) // 2)

        def over_chunks_unrolled(eng, step):
            for c in range(NCH):
                step(c, c % 2, c // 2)

        def is_chunk(c):
            return not isinstance(c, int) or c < NCH

        def over_steps(eng, step, lags):
            for k in range(2 * U):
                step(k, k % U, k)
            with eng.Fori(2, NG // U) as i:
                for u in range(U):
                    step(i * U + u, u, i)
            for k in range(NG, NG + lags):
                step(k, k % U, k)

        def has(k, lag):
            return not isinstance(k, int) or 0 <= k - lag < NG

        def rows_written(eng, n, c):
            eng.wait_ge(node[n]["rows"], c + 1)
            if n != 1:
                eng.wait_ge(node[n]["rows_v"], c + 1)

        def table_stored(eng, m):
            eng.wait_ge(tables, m + 1)

        def node_blocks(eng, step, first, hook, done):
            def block(c, start, rounds):
                for h in range(2 * U):
                    step((start + h // U) * U + h % U, h % U, start + h // U)
                    hook(c, h)
                if rounds > 2:
                    with eng.Fori(2, rounds) as r:
                        for u in range(U):
                            step((start + r) * U + u, u, start + r)
            with eng.Fori(0, NCH - 2) as c:
                block(c, c * BR + first, BR)
                done(c)
            start = first + (NCH - 2) * BR
            block(NCH - 2, start, NG // U - start)

        def over_steps_and_chunks(eng, step, hook, done, lags, last_steps):
            for k in range(2 * U):
                step(k, k % U, k)
            with eng.Fori(2, NODE_ROUND) as i:
                for u in range(U):
                    step(i * U + u, u, i)
            node_blocks(eng, step, NODE_ROUND, hook, done)
            for k in range(NG, NG + lags):
                step(k, k % U, k)
                last_steps(k)

        def until_stored(eng, n):
            return lambda c: eng.wait_ge(stored[n + 1][0], 16 * (c + 1))

        block = ctx.enter_context(nc.Block())

        @block.sync
        def _(sp):
            def one(dst_ap, src_ap, semaphore):
                sp.dma_start(dst_ap, src_ap).then_inc(semaphore, 16)

            def load_rows(semaphore, frm, c, u):
                sp.dma_start(xs[:, u, :, :], frm[bass.ds(c * CN, CN), :].rearrange("(t p) f -> p t f", p=P)).then_inc(semaphore, 16)

            def store_rows(m, to, c, u):
                if isinstance(c, int) and c == NCH - 1 and to.shape[0] < NP:
                    sp.dma_start(to[c * CN:c * CN + (CT - 1) * P, :].rearrange("(t p) f -> p t f", p=P),
                                 done_rows[:, u, 0:CT - 1, :]).then_inc(stored[m][u], 16)
                    sp.dma_start(to[N - TAIL:N, :], done_rows[0:TAIL, u, CT - 1, :]).then_inc(stored[m][u], 16)
                else:
                    sp.dma_start(to[bass.ds(c * CN, CN), :].rearrange("(t p) f -> p t f", p=P),
                                 done_rows[:, u, :, :]).then_inc(stored[m][u], 16)

            def load_x(c):
                tiles = CT - (c == NCH - 1)
                sp.dma_start(x_rows[:, c * CT:c * CT + tiles, :],
                             x[c * CN:c * CN + tiles * P, :].rearrange("(t p) f -> p t f", p=P)).then_inc(x_in[c], 16)
            load_x(0)
            one(wn1[:, :, :], Wn1.rearrange("(a k) n -> k a n", a=2), s["first_weights"])
            one(bias_rows[:, 0, :], bn1.rearrange("(a n) -> a n", a=1).to_broadcast((P, P)), s["first_weights"])
            load_x(1)
            sp.wait_ge(s["edge_pads"], 4)
            full = (NG - 1 - P) // 64 * 64
            for to, frm, got in ((src_i, src, "src_in"), (dst_i, dst, "dst_in")):
                one(to[:, 0, :], frm[0:P * GE].rearrange("(q e) -> q e", e=GE), s[got])
                one(to[0:full, 1, :], frm[P * GE:(P + full) * GE].rearrange("(q e) -> q e", e=GE), s[got])
                one(to[full:NG - 1 - P, 1, :], frm[(P + full) * GE:(NG - 1) * GE].rearrange("(q e) -> q e", e=GE), s[got])
                one(to[NG - 1 - P:NG - P, 1, :], frm[LAST:E].rearrange("(q e) -> q e", e=GE), s[got])
                load_x(2 if to is src_i else 3)
            for c in range(4, NCH):
                load_x(c)
            sp.dma_start(x_rows[0:TAIL, NT - 1, :], x[N - TAIL:N, :]).then_inc(x_in[NCH - 1], 16)
            weights = [(w[:, :], d) for w, d in ((we1[0:CH, 0, :], We1), (we1[CH:2 * CH, 1, :], We1), (we2, We2), (wn2, Wn2),
                                                 (wr[0], Wr0), (wr[1], Wr1), (wo[0], Wo0), (wo[1], Wo1))]
            weights += [(bias_rows[:, m, :], v.rearrange("(a n) -> a n", a=1).to_broadcast((P, P))) for m, v in ((1, br0), (2, br1))]
            weights += [(bn2_row[:, :], bn2.rearrange("(a n) -> a n", a=1))]
            weights += [(cols[:, i:i + 1], Wt.rearrange("a n -> n a") if v is None else v.rearrange("(n a) -> n a", a=1))
                        for i, v in enumerate((be1, be2, None, bt))]
            for c in range(NCH):
                for w, d in weights[3 * c:3 * c + 3]:
                    one(w, d, s["weights"])
                sp.wait_ge(proj[0]["rows"], c + 1)
                store_rows(0, table[0], c, c % 2)

            def edges(g, u, i):
                wait(sp, s["attrs_turned"], g - U + 1)
                first = LAST if isinstance(g, int) and g == NG - 1 else g * GE
                sp.dma_start(ea[:, u, :, :], edge_attr[bass.ds(first, GE), :].rearrange("(p j) c -> p j c", j=TPG)).then_inc(ea_in[u], 16)
                wait_alone(sp, s["time_weights"], g - U + 1)
                sp.dma_start(tsb[:, u, :], edge_time[bass.ds(first, GE)].rearrange("(a e) -> a e", a=1).to_broadcast((P, GE))).then_inc(ts_in[u], 16)
            for g in range(U):
                edges(g, g, g)
            sp.wait_ge(stored[0][0], 16 * (NCH // 2 + 1))
            sp.wait_ge(stored[0][1], 16 * (NCH // 2))
            sp.sem_inc(tables, 1)

            def own_loads(m):
                def load_own(c, m=m):
                    wait(sp, proj[m]["rows"], c)
                    load_rows(proj[m]["loaded"], table[m], c, 0)
                    if m == 2:
                        load_rows(proj[m]["x1_loaded"], table[1], c, 1)
                load_own(0)
                with sp.Fori(1, NCH) as c:
                    load_own(c)

            def store(n, c, u):
                rows_written(sp, n, c)
                store_rows(n + 1, table[n + 1] if n < 2 else out, c, u)

            def store_last(n, t):
                rows_written(sp, n, NCH - 1 + t)
                (a, b), to = SPAN[t], table[n + 1] if n < 2 else out
                whole = b - (t == 1 and n == 2)
                first = (NCH - 1) * CN
                sp.dma_start(to[first + a * P:first + whole * P, :].rearrange("(t p) f -> p t f", p=P),
                             done_rows[:, 1, a:whole, :]).then_inc(stored[n + 1][1], 16)
                if whole < b:
                    sp.dma_start(to[N - TAIL:N, :], done_rows[0:TAIL, 1, CT - 1, :]).then_inc(stored[n + 1][1], 16)

            def any_order():
                with sp.Fori(1, NG // U - 1) as i:
                    for u in range(U):
                        edges(i * U + u, u, i)
                for g in range(NG - U, NG):
                    edges(g, g % U, g)
                for n in range(NPH):
                    if n > 0:
                        own_loads(n)
                    over_chunks(sp, lambda c, u, i: store(n, c, u))
                    sp.wait_ge(stored[n + 1][0], 16 * (NCH // 2 + 1 + (n == 2)))
                    sp.wait_ge(stored[n + 1][1], 16 * (NCH // 2))
                    sp.sem_inc(tables, 1)

            def sorted_order():
                at = NODE_ROUND + 2

                def rounds(eng_range, start):
                    with sp.Fori(*eng_range) as r:
                        for u in range(U):
                            edges((start + r) * U + u, u, start + r)
                rounds((1, at), 0)
                with sp.Fori(0, NCH - 3) as c:
                    store(0, c, 0)
                    rounds((0, BR), c * BR + at)
                store(0, NCH - 3, 0)
                rounds((at + (NCH - 3) * BR, NG // U - 1), 0)
                for g in range(NG - U, NG):
                    edges(g, g % U, g)
                store(0, NCH - 2, 0)
                for n in range(NPH):
                    if n > 0:
                        own_loads(n)
                        with sp.Fori(0, NCH - 1) as c:
                            store(n, c, 0)
                    for t in BOTH:
                        store_last(n, t)
                    sp.wait_ge(stored[n + 1][0], 16 * (NCH - 1))
                    sp.wait_ge(stored[n + 1][1], 16 * (2 + (n == 2)))
                    sp.sem_inc(tables, 1)

            sp.wait_ge(s["lists_ready"], 1)
            spread = sp.value_load(flag[0:1, 0:1], min_val=0, max_val=1)
            with sp.If(spread == 0):
                sorted_order()
            with sp.Else():
                any_order()

        @block.gpsimd
        def _(pool):
            nc.gpsimd.memset(dst_i[:, 1, :], N).then_inc(s["edge_pads"], 1)
            nc.gpsimd.memset(src_i[:, 1, :], 0).then_inc(s["edge_pads"], 1)
            nc.gpsimd.memset(x_rows[:, NT - 1, :], 0.0).then_inc(s["edge_pads"], 1)
            nc.gpsimd.memset(we1[:, :, :], 0.0).then_inc(s["edge_pads"], 1)
            nc.gpsimd.memset(ident[:, :], 0.0).then_inc(s["ident_zero"], 1)
            pool.wait_ge(s["ident_zero"], 1)
            nc.gpsimd.affine_select(out=ident[:, :], in_=ident[:, :], compare_op=ALU.not_equal, fill=1.0, base=0,
                                    pattern=[[-1, P]], channel_multiplier=1).then_inc(s["consts"], 1)
            nc.gpsimd.memset(ones[:, :], 1.0).then_inc(s["consts"], 1)
            nc.gpsimd.memset(ones16[:, :], 1.0).then_inc(s["consts"], 1)
            nc.gpsimd.iota(iota[:, :], pattern=[[1, WN]], base=0, channel_multiplier=0,
                           allow_small_or_imprecise_dtypes=True).then_inc(s["consts"], 1)
            nc.gpsimd.iota(win_base[:, :], pattern=[[WN, NWIN]], base=0, channel_multiplier=0,
                           allow_small_or_imprecise_dtypes=True).then_inc(s["consts"], 1)
            nc.gpsimd.iota(past_due[:, :, NCH - 1], pattern=[[P, HALVES]], base=1 - LAST_DUE, channel_multiplier=1,
                           allow_small_or_imprecise_dtypes=True).then_inc(s["consts"], 1)
            nc.gpsimd.iota(past_due[:, :, 0:NCH - 1], pattern=[[P, HALVES], [-BR * U, NCH - 1]], base=1 + LAG - NODE_ROUND * U, channel_multiplier=1,
                           allow_small_or_imprecise_dtypes=True).then_inc(s["consts"], 1)
            nc.gpsimd.memset(eps_c[:, :], EPS).then_inc(s["consts"], 1)
            for a in (acc_a, degree):
                nc.gpsimd.memset(a[:, :], 0.0).then_inc(s["zeroed"], 1)
            pool.wait_ge(s["prep"], 1)
            q = NG - 1 - P
            nc.gpsimd.affine_select(out=dst_g[:, 1, :], in_=dst_g[:, 1, :], compare_op=ALU.is_ge, fill=NOWHERE,
                                    base=GE * 2 * q - REPEATED, pattern=[[1, GE]], channel_multiplier=-GE * 2).then_inc(s["masked"], 1)

            for ph in range(NPH):
                table_stored(pool, ph)

                def group(g, u, i, ph=ph):
                    pool.wait_ge(s["idx_ready"], ph * NG + g + 1)
                    if ph == 0:
                        wait_alone(pool, s["message_summed"], g - U + 1)
                    elif not isinstance(g, int) or g >= U:
                        wait_alone(pool, s["window_summed"], ph * NG + g - U + 1)
                    for j in range(TPG):
                        nc.gpsimd.indirect_dma_start(
                            rows[:, u, j, :], None, table[ph][:, :],
                            bass.IndirectOffsetOnAxis(ap=idx[:, u, j:j + 1], axis=0)).then_inc(gathered[u], 16)
                for g in range(U):
                    group(g, g, 0)
                with pool.Fori(1, NG // U) as i:
                    for u in range(U):
                        group(i * U + u, u, i)

        @block.scalar
        def _(act):
            def stage_idx(ph, g, u, i):
                if not (isinstance(g, int) and g < U):
                    before = ph * (NG // U) + (g // U if isinstance(g, int) else i)
                    act.wait_ge(gathered[u], 16 * TPG * before)
                nc.scalar.copy(idx[:, u, :], src_idx[:, bass.ds(g * TPG, TPG)]).then_inc(s["idx_ready"], 1)

            def turn(m, c, u):
                act.wait_ge(proj[m]["turned"], c + 1)
                wait(act, proj[m]["product"], c - 1 if m == 0 else c)
                for t in range(2):
                    last = nc.scalar.copy(fm[:, u, in_fm(t)], turned_in(u)[t][:, 0:width(t)])
                last.then_inc(proj[m]["fm"], 1)

            turn(0, 0, 0)
            turn(0, 1, 1)
            act.wait_ge(s["src_in"], 64)
            nc.scalar.copy(src_g[:, :, :], src_i[:, :, :]).then_inc(s["src_cast"], 1)
            with act.Fori(1, NCH // 2) as i:
                for u in range(2):
                    turn(0, 2 * i + u, u)
            turn(0, NCH - 1, 0)
            act.wait_ge(s["src_ready"], 1)
            for g in range(U):
                stage_idx(0, g, g, 0)
            act.wait_ge(s["weights"], 16 * 15)
            act.wait_ge(s["lists_ready"], 1)

            def step(k, u, i):
                if has(k, 0) and not (isinstance(k, int) and k < U):
                    stage_idx(0, k, u, i)
                if has(k, 1):
                    g = k - 1
                    act.wait_ge(s["hidden_product"], g + 1)
                    wait(act, s["features_product"], g - 1)
                    nc.scalar.activation(h1[:, (u - 1) % 2, :], ps_h[:, :], ACT.Relu, bias=be1_c).then_inc(s["hidden_ready"], 1)
                if has(k, 2):
                    g = k - 2
                    v = (u - 2) % U
                    use = g // U + 1 if isinstance(g, int) else (i + 1 if u >= 2 else i)
                    act.wait_ge(ts_in[v], 16 * use)
                    wait(act, s["features_ready"], g - 1)
                    nc.scalar.activation(tw[:, v % 2, :].rearrange("f (j p) -> f j p", j=TPG),
                                         tsb[:, v, :].rearrange("f (p j) -> f j p", j=TPG),
                                         ACT.Sigmoid, scale=wt_c, bias=bt_c).then_inc(s["time_weights"], 1)
                if has(k, 3):
                    g = k - 3
                    act.wait_ge(s["message_summed"], g + 1)
                    m = msg[:, (u - 3) % 2, :, :]
                    nc.scalar.activation(m, m, ACT.Relu).then_inc(s["message_ready"], 1)
            def deviations(n, c, v, ts=BOTH):
                a, _, b = tiles_of(ts)
                act.wait_ge(node[n]["mv"], c + 1)
                nc.scalar.activation(std[:, v, a:b], mv[:, v, a:b, 1], ACT.Sqrt, bias=eps_c[:, :]).then_inc(node[n]["std"], 1)

            def norm(n, c, u, i, next_too=True, ts=BOTH):
                act.wait_ge(node[n]["shift"], c + 1)
                wait(act, stored[n + 1][u], 16 * i)
                for j in range(*tiles_of(ts)[1:]):
                    last = nc.scalar.activation(done_rows[:, u, j, :], nm[:, u, j, :], ACT.Identity,
                                                scale=rstd[:, u, j:j + 1], bias=shift[:, u, j:j + 1])
                last.then_inc(node[n]["rows"], 1)
                if next_too and is_chunk(c + 1):
                    deviations(n, c + 1, (u + 1) % 2)

            def relu(c, u, i, ts=BOTH):
                a, _, b = tiles_of(ts)
                act.wait_ge(node[1]["added"], c + 1)
                wait(act, stored[2][u], 16 * i)
                nc.scalar.activation(done_rows[:, u, a:b, :], nm[:, u, a:b, :], ACT.Relu).then_inc(node[1]["rows"], 1)

            def hook_of(n):
                def hook(c, h):
                    if n == 0 and h == 0:
                        act.wait_ge(s["window_added"], (c * BR + NODE_ROUND) * U - LAG)
                        nc.scalar.copy(fm[:, 0, :], acc_a[:, bass.ds(c * CN, CN)])
                        nc.scalar.copy(fm[0:1, 1, :], degree[0:1, bass.ds(c * CN, CN)]).then_inc(node[0]["lhs"], 1)
                    if n == 1 and h == 3:
                        relu(c, 0, 0)
                    if n != 1 and h == 4:
                        deviations(n, c, 0)
                    if n != 1 and h == 5:
                        norm(n, c, 0, 0, False)
                return hook

            def last_chunk(n):
                for t in BOTH:
                    c = NCH - 1 + t
                    if n == 1:
                        relu(c, 1, 0, (t,))
                    else:
                        deviations(n, c, 1, (t,))
                        norm(n, c, 1, 0, False, (t,))

            def all_phases(general):
                table_stored(act, 0)
                if general:
                    over_steps(act, step, 5)
                    deviations(0, 0, 0)
                    over_chunks(act, lambda c, u, i: norm(0, c, u, i))
                else:
                    over_steps_and_chunks(act, step, hook_of(0), until_stored(act, 0), 5, lambda k: None)
                    last_chunk(0)

                for ph in (1, 2):
                    for g in range(U):
                        act.wait_ge(gathered[g], 16 * TPG * ph * (NG // U))
                        nc.scalar.copy(idx[:, g, :], src_idx[:, g * TPG:(g + 1) * TPG]).then_inc(s["idx_ready"], 1)
                    for g in range(U, 2 * U):
                        stage_idx(ph, g, g - U, 1)
                    def two_rounds(c, ph=ph):
                        for i in (2 * c + 2, 2 * c + 3):
                            for u in range(U):
                                stage_idx(ph, i * U + u, u, i)
                        turn(ph, c, 0)
                    two_rounds(0)
                    with act.Fori(1, NCH) as c:
                        two_rounds(c)
                    ahead = NG // U if general else NODE_ROUND + 1
                    with act.Fori(2 * NCH + 2, ahead) as i:
                        for u in range(U):
                            stage_idx(ph, i * U + u, u, i)
                    if not general:
                        def stage(k, u, i, ph=ph):
                            if has(k, 0):
                                stage_idx(ph, k, u, i)
                        node_blocks(act, stage, ahead, hook_of(ph), until_stored(act, ph))
                        last_chunk(ph)
                        continue
                    table_stored(act, ph)
                    if ph == 1:
                        over_chunks(act, relu)
                    else:
                        deviations(2, 0, 0)
                        over_chunks(act, lambda c, u, i: norm(2, c, u, i))

            spread = act.value_load(flag[0:1, 0:1], min_val=0, max_val=1)
            with act.If(spread == 0):
                all_phases(False)
            with act.Else():
                all_phases(True)

        @block.tensor
        def _(pe):
            def transposes(dst_banks, src_of):
                for t in range(2):
                    for j in range(*SPAN[t]):
                        o = (j - SPAN[t][0]) * P
                        last = nc.tensor.transpose(dst_banks[t][:, o:o + P], src_of(j), ident[:, :])
                return last

            pe.wait_ge(s["consts"], 8)
            pe.wait_ge(s["first_weights"], 32)

            def turn(m, c, u, rows_ap):
                wait(pe, proj[m]["fm"], c - 1 if m == 0 else c)
                transposes(turned_in(u), rows_ap).then_inc(proj[m]["turned"], 1)

            def product(m, c, u, w):
                pe.wait_ge(proj[m]["fm"], c + 1)
                for t in range(2):
                    wait(pe, proj[m]["rows" if t else "bank"], c)
                    for j in range(*SPAN[t]):
                        o = (j - SPAN[t][0]) * P
                        last = nc.tensor.matmul(pair(1)[t][:, o:o + P], fm[:, u, j * P:(j + 1) * P], w, start=True, stop=True)
                last.then_inc(proj[m]["product"], 1)

            def turn_lists(lists, banks, signal):
                for h in range(HALVES):
                    for j in range(TPG):
                        v = lists[:, h, :].rearrange("q (p j) -> q j p", j=TPG)[:, j, :]
                        last = nc.tensor.transpose(banks[h][:, j * P:(j + 1) * P], v, ident[:, :])
                last.then_inc(signal, 1)

            def turn_x(c):
                pe.wait_ge(x_in[c], 32 if c == NCH - 1 else 16)
                turn(0, c, c % 2, lambda j: x_rows[:, c * CT + j, :])
            turn_x(0)
            turn_x(1)
            for c in range(NCH):
                product(0, c, c % 2, wn1[:, 0, :])
                if c + 2 < NCH:
                    turn_x(c + 2)
                if c == 2:
                    pe.wait_ge(s["src_cast"], 1)
                    turn_lists(src_g, pair(2), s["src_turned"])
                if c == 4:
                    pe.wait_ge(s["masked"], 1)
                    pe.wait_ge(s["src_ready"], 1)
                    turn_lists(dst_g, pair(2), s["dst_turned"])

            pe.wait_ge(s["prep"], 2)
            nc.tensor.transpose(B[0][0:1, 0:P], over1[:, :], ident[:, :])
            for h in range(HALVES):
                nc.tensor.transpose(B[0][0:1, (h + 1) * P:(h + 2) * P], base[:, h:h + 1], ident[:, :])
            for h in range(HALVES):
                last = nc.tensor.matmul(B[1][:, h * P:(h + 1) * P], ones[:, :], diag[:, h, :], start=True, stop=True)
            last.then_inc(s["bounds"], 1)
            pe.wait_ge(s["weights"], 16 * 15)
            pe.wait_ge(s["lists_ready"], 1)

            def segment_sum(ph, k, lag, u, i, general):
                g = k - lag
                v = (u - lag) % U
                seq = ph * NG + g
                if ph == 0:
                    wait_alone(pe, s["message_ready"], g + 1)
                    data = msg[:, v % 2, :, :]
                else:
                    use = ph * (NG // U) + (g // U + 1 if isinstance(g, int) else (i + 1))
                    wait_alone(pe, gathered[v], 16 * TPG * use)
                    data = rows[:, v, :, :]

                def window(oh, signal):
                    if ph == 0:
                        for j in range(TPG):
                            half = oh[:, j, :].bitcast(bf16).rearrange("p (n t) -> p t n", t=2)[:, 1, :]
                            nc.tensor.matmul(ps_d[:, 0:WN], ones16[:, :], half, start=(j == 0), stop=(j == TPG - 1))
                    for j in range(TPG):
                        last = nc.tensor.matmul(ps_s[:, 0:WN], data[:, j, :], oh[:, j, :], start=(j == 0), stop=(j == TPG - 1))
                    last.then_inc(signal, 1)
                if general:
                    oh = onehot[:, 0, :, :]
                    with pe.Fori(0, NWIN - 1) as w:
                        pe.wait_ge(s["any_onehots"], seq * NWIN + w + 1)
                        window(oh, s["any_summed"])
                    pe.wait_ge(s["any_onehots"], seq * NWIN + NWIN)
                    window(oh, s["window_summed"])
                else:
                    pe.wait_ge(s["onehots_ready"], seq + 1)
                    wait(pe, s["window_added"], seq)
                    window(onehot[:, v % 2, :, :], s["window_summed"])

            def step_of(general):
                def step(k, u, i):
                    if has(k, 0):
                        use = k // U + 1 if isinstance(k, int) else i + 1
                        pe.wait_ge(ea_in[u], 16 * use)
                        wait_alone(pe, s["attrs_copied"], k)
                        for q in range(TPG // 2):
                            pair_of = ea[:, u, 2 * q:2 * q + 2, :].rearrange("p j c -> p (j c)")
                            last = nc.tensor.transpose(ps_t[:, q * P:(q + 1) * P], pair_of, ident[:, :])
                        last.then_inc(s["attrs_turned"], 1)
                    if has(k, 1):
                        g = k - 1
                        pe.wait_ge(s["attrs_copied"], g + 1)
                        wait(pe, s["hidden_ready"], g)
                        for odd in range(2):
                            to = ps_h[:, :].rearrange("f (q o p) -> f q o p", o=2, p=P)
                            last = nc.tensor.matmul(to[:, :, odd, :], we1[:, odd, :],
                                                    eaT[:, (u - 1) % 2, :].rearrange("c (q p) -> c q p", p=P), start=True, stop=True)
                        last.then_inc(s["hidden_product"], 1)
                    if has(k, 2):
                        g = k - 2
                        pe.wait_ge(s["hidden_ready"], g + 1)
                        wait(pe, s["features_ready"], g)
                        nc.tensor.matmul(ps_e[:, :], we2[:, :], h1[:, (u - 2) % 2, :], start=True, stop=True).then_inc(s["features_product"], 1)
                    if has(k, 3):
                        g = k - 3
                        pe.wait_ge(s["features_ready"], g + 1)
                        wait(pe, s["message_summed"], g)
                        for j in range(TPG):
                            last = nc.tensor.matmul(ps_z[:, j * P:(j + 1) * P], efT[:, (u - 3) % 2, j * P:(j + 1) * P],
                                                    wn1[:, 1, :], start=True, stop=True)
                        last.then_inc(s["message_product"], 1)
                    if has(k, 4):
                        segment_sum(0, k, 4, u, i, general)
                return step

            def node_products(n):
                def chunk(c, u, i):
                    pe.wait_ge(node[n]["lhs"], c + 1)
                    wait(pe, node[n]["added"], c - 1)
                    for t in range(2):
                        for j in range(*SPAN[t]):
                            o = (j - SPAN[t][0]) * P
                            last = nc.tensor.matmul(pair(u)[t][:, o:o + P], fm[:, u, j * P:(j + 1) * P], wr[n - 1][:, :],
                                                    start=True, stop=True)
                    last.then_inc(node[n]["product"], 1)
                return chunk

            def message_products(c, u, i):
                wait(pe, node[0]["added"], c - 1)
                for t in range(2):
                    for j in range(*SPAN[t]):
                        at = pair(u)[t][:, (j - SPAN[t][0]) * P:(j - SPAN[t][0] + 1) * P]
                        nodes_of = slice(c * CN + j * P, c * CN + (j + 1) * P)
                        nc.tensor.matmul(at, acc_a[:, nodes_of], wn2[:, :], start=True, stop=False)
                        last = nc.tensor.matmul(at, degree[0:1, nodes_of], bn2_row[:, :], start=False, stop=True)
                last.then_inc(node[0]["product"], 1)

            def chunk_products(n, c, u, ts=BOTH):
                if n > 0 or u == 0:
                    pe.wait_ge(node[n]["lhs"], c + 1)
                for t in ts:
                    for j in range(*SPAN[t]):
                        at = pair(3)[t][:, (j - SPAN[t][0]) * P:(j - SPAN[t][0] + 1) * P]
                        if n > 0:
                            last = nc.tensor.matmul(at, fm[:, u, j * P:(j + 1) * P], wr[n - 1][:, :], start=True, stop=True)
                            continue
                        if u == 0:
                            sums, degrees = fm[:, 0, j * P:(j + 1) * P], fm[0:1, 1, j * P:(j + 1) * P]
                        else:
                            nodes_of = slice((NCH - 1) * CN + j * P, (NCH - 1) * CN + (j + 1) * P)
                            sums, degrees = acc_a[:, nodes_of], degree[0:1, nodes_of]
                        nc.tensor.matmul(at, sums, wn2[:, :], start=True, stop=False)
                        last = nc.tensor.matmul(at, degrees, bn2_row[:, :], start=False, stop=True)
                last.then_inc(node[n]["product"], 1)

            def hook_of(n):
                def hook(c, h):
                    if h == 1:
                        chunk_products(n, c, 0)
                    if n > 0 and h == 2 * U - 2 and isinstance(c, int):
                        chunk_products(n, NCH - 1, 1, (0,))
                return hook

            def all_phases(general):
                if general:
                    over_steps(pe, step_of(True), 5)
                    pe.wait_ge(s["window_added"], NG)
                    over_chunks_unrolled(pe, message_products)
                else:
                    def last_steps(k):
                        if k == NG + 2:
                            pe.wait_ge(s["window_added"], LAST_DUE)
                            chunk_products(0, NCH - 1, 1, (0,))
                    over_steps_and_chunks(pe, step_of(False), hook_of(0), lambda c: None, 5, last_steps)
                    pe.wait_ge(s["window_added"], NG)
                    chunk_products(0, NCH, 1, (1,))
                for ph in (1, 2):
                    def step(k, u, i, ph=ph):
                        segment_sum(ph, k, 0, u, i, general)
                    pe.wait_ge(node[ph - 1]["added"], NCH + (not general))
                    for g in range(U):
                        step(g, g, 0)
                    def two_rounds(c, ph=ph, step=step):
                        for i in (2 * c + 1, 2 * c + 2):
                            for u in range(U):
                                step(i * U + u, u, i)
                        pe.wait_ge(proj[ph]["loaded"], 16 * (c + 1))
                        turn(ph, c, 0, lambda j: xs[:, 0, j, :])
                        product(ph, c, 0, wo[ph - 1][:, :])
                    two_rounds(0)
                    with pe.Fori(1, NCH) as c:
                        two_rounds(c)
                    with pe.Fori(2 * NCH + 1, NG // U if general else NODE_ROUND) as i:
                        for u in range(U):
                            step(i * U + u, u, i)
                    if general:
                        pe.wait_ge(proj[ph]["rows"], NCH)
                        over_chunks(pe, node_products(ph))
                    else:
                        node_blocks(pe, step, NODE_ROUND, hook_of(ph), lambda c: None)
                        chunk_products(ph, NCH, 1, (1,))

            spread = pe.value_load(flag[0:1, 0:1], min_val=0, max_val=1)
            with pe.If(spread == 0):
                all_phases(False)
            with pe.Else():
                all_phases(True)

        @block.vector
        def _(dve):
            steps = [0]

            def link(ins):
                steps[0] += 1
                ins.then_inc(s["link"], 1)
                dve.wait_ge(s["link"], steps[0])

            def project(m, c, u, before):
                dve.wait_ge(proj[m]["product"], c + 1)
                if m == 0:
                    wait(dve, stored[0][u], 16 * before)
                for t in range(2):
                    a, b = SPAN[t]
                    to = done_rows[:, u, a:b, :] if m == 0 else own[:, bass.ds(c * CT + a, b - a), :] if m == 1 else nm[:, 0, a:b, :]
                    last = nc.vector.tensor_tensor(to, as_rows(pair(1)[t], t),
                                                   bias_rows[:, m:m + 1, :].to_broadcast((P, b - a, F)), ALU.add)
                    if t == 0:
                        last.then_inc(proj[m]["bank"], 1)
                if m == 2:
                    last.then_inc(s["own_part"], 1)
                    dve.wait_ge(s["own_part"], c + 1)
                    dve.wait_ge(proj[2]["x1_loaded"], 16 * (c + 1))
                    last = nc.vector.tensor_tensor(own[:, bass.ds(c * CT, CT), :], nm[:, 0, :, :], xs[:, 1, :, :], ALU.add)
                last.then_inc(proj[m]["rows"], 1)

            def copy_list(to_all, h):
                to = to_all[:, h * P * TPG:(h + 1) * P * TPG].rearrange("p (q j) -> p q j", j=TPG)
                return nc.vector.tensor_copy(to, pair(2)[h][:, :].rearrange("p (j q) -> p q j", j=TPG))

            dve.wait_ge(s["dst_in"], 16 * 4)
            link(nc.vector.tensor_copy(dst_g[:, :, :], dst_i[:, :, :]))
            dve.wait_ge(s["first_weights"], 32)
            project(0, 0, 0, 0)
            nc.vector.tensor_reduce(lo[:, :], dst_g[:, :, :], AX.X, ALU.min)
            project(0, 1, 1, 0)
            nc.vector.tensor_reduce(hi[:, :], dst_g[:, :, :], AX.X, ALU.max).then_inc(s["prep"], 1)
            project(0, 2, 0, 1)
            dve.wait_ge(s["src_turned"], 1)
            for h in range(HALVES):
                last = copy_list(src_idx, h)
            last.then_inc(s["src_ready"], 1)
            project(0, 3, 1, 1)
            dve.wait_ge(s["prep"], 1)
            link(nc.vector.tensor_scalar(base[:, :], lo[:, :], float(NP - WN), None, ALU.min))
            link(nc.vector.tensor_tensor(over[:, :], hi[:, :], base[:, :], ALU.subtract))
            dve.wait_ge(s["consts"], 8)
            nc.vector.tensor_scalar(past_due[:, :, NCH - 1], past_due[:, :, NCH - 1], 0.0, float(width(0)), ALU.is_gt, ALU.mult)
            link(nc.vector.tensor_scalar(past_due[:, :, 0:NCH - 1], past_due[:, :, 0:NCH - 1], 0.0, float(CN), ALU.is_gt, ALU.mult))
            project(0, 4, 0, 2)
            link(nc.vector.tensor_reduce(due[:, :], past_due[:, :, :], AX.X, ALU.add))
            link(nc.vector.scalar_tensor_tensor(out=late[:, :], in0=due[:, :], scalar=float(WN - 1), in1=lo[:, :],
                                                op0=ALU.add, op1=ALU.subtract))
            link(nc.vector.tensor_tensor(over[:, :], over[:, :], late[:, :], ALU.max))
            nc.vector.tensor_reduce(over1[:, :], over[:, :], AX.X, ALU.max)
            for h in range(HALVES):
                last = nc.vector.tensor_scalar(diag[:, h, :], ident[:, :], base[:, h:h + 1], None, ALU.mult)
            last.then_inc(s["prep"], 1)
            project(0, 5, 1, 2)
            dve.wait_ge(s["dst_turned"], 1)
            for h in range(HALVES):
                last = copy_list(dst_abs, h)
            link(last)
            project(0, 6, 0, 3)
            dve.wait_ge(s["bounds"], 1)
            link(nc.vector.tensor_reduce(over_f[:, :], B[0][0:1, 0:P], AX.X, ALU.max))
            nc.vector.tensor_scalar(flag[:, :], over_f[:, :], float(WN), None, ALU.is_ge)
            nc.vector.tensor_copy(base_row[:, :], B[0][0:1, P:(1 + HALVES) * P])
            for h in range(HALVES):
                to, frm = (a[:, h * P * TPG:(h + 1) * P * TPG].rearrange("p (q j) -> p q j", j=TPG) for a in (dst_rel, dst_abs))
                for j in range(TPG):
                    last = nc.vector.tensor_tensor(to[:, :, j], frm[:, :, j], B[1][:, h * P:(h + 1) * P], ALU.subtract)
            last.then_inc(s["lists_ready"], 1)
            dve.wait_ge(s["lists_ready"], 1)
            dve.wait_ge(s["weights"], 16 * 15)

            dve.wait_ge(s["zeroed"], 2)

            def one_hots(cols_ap, v, signal):
                for j in range(TPG):
                    last = nc.vector.tensor_scalar(onehot[:, v, j, :], iota[:, :], cols_ap(j), None, ALU.is_equal)
                last.then_inc(signal, 1)

            def fast_one_hots(ph, g, v):
                wait(dve, s["window_summed"], ph * NG + g - 1)
                one_hots(lambda j: dst_rel[:, bass.ds(g * TPG + j, 1)], v % 2, s["onehots_ready"])

            def fast_add(ph, g, at):
                seq = ph * NG + g
                dve.wait_ge(s["window_summed"], seq + 1)
                wait(dve, s["window_added"], seq)
                if ph == 0:
                    o = degree[:, bass.ds(at, WN)]
                    nc.vector.tensor_tensor(o, o, ps_d[:, 0:WN], ALU.add)
                o = acc[ph][:, bass.ds(at, WN)]
                nc.vector.tensor_tensor(o, o, ps_s[:, 0:WN], ALU.add).then_inc(s["window_added"], 1)

            def base_of(g):
                return dve.value_load(base_row[0:1, bass.ds(g, 1)], min_val=0, max_val=NP - WN)

            def all_windows(ph, g):
                seq = ph * NG + g

                def window(w, at, signal, value):
                    nc.vector.tensor_scalar(rel_w[:, :], dst_abs[:, bass.ds(g * TPG, TPG)], win_base[:, bass.ds(w, 1)], None,
                                            ALU.subtract).then_inc(s["any_relative"], 1)
                    dve.wait_ge(s["any_relative"], seq * NWIN + w + 1)
                    one_hots(lambda j: rel_w[:, j:j + 1], 0, s["any_onehots"])
                    dve.wait_ge(signal, value)
                    if ph == 0:
                        o = degree[:, bass.ds(at, WN)]
                        nc.vector.tensor_tensor(o, o, ps_d[:, 0:WN], ALU.add)
                    o = acc[ph][:, bass.ds(at, WN)]
                    nc.vector.tensor_tensor(o, o, ps_s[:, 0:WN], ALU.add).then_inc(s["any_added"], 1)
                    dve.wait_ge(s["any_added"], seq * NWIN + w + 1)
                with dve.Fori(0, NWIN - 1) as w:
                    window(w, w * WN, s["any_summed"], seq * (NWIN - 1) + w + 1)
                window(NWIN - 1, (NWIN - 1) * WN, s["window_summed"], seq + 1)
                dve.sem_inc(s["window_added"], 1)

            def step_of(general):
                def step(k, u, i):
                    if has(k, 0):
                        dve.wait_ge(s["attrs_turned"], k + 1)
                        wait(dve, s["hidden_product"], k - 1)
                        nc.vector.tensor_copy(eaT[:, u % 2, :], ps_t[:, 0:GE // 2]).then_inc(s["attrs_copied"], 1)
                    if not general and has(k, 5):
                        fast_add(0, k - 5, base_of(k - 5))
                    if not general and has(k, 3):
                        fast_one_hots(0, k - 3, u - 3)
                    if has(k, 2):
                        g = k - 2
                        dve.wait_ge(s["features_product"], g + 1)
                        dve.wait_ge(s["time_weights"], g + 1)
                        wait(dve, s["message_product"], g - 1)
                        nc.vector.scalar_tensor_tensor(out=efT[:, u % 2, :], in0=ps_e[:, :], scalar=be2_c, in1=tw[:, u % 2, :],
                                                       op0=ALU.add, op1=ALU.mult).then_inc(s["features_ready"], 1)
                    if has(k, 3):
                        g = k - 3
                        v = (u - 3) % U
                        use = g // U + 1 if isinstance(g, int) else (i + 1 if u == 3 else i)
                        dve.wait_ge(s["message_product"], g + 1)
                        dve.wait_ge(gathered[v], 16 * TPG * use)
                        wait(dve, s["window_summed"], g - 1)
                        nc.vector.tensor_tensor(msg[:, v % 2, :, :], ps_z[:, :].rearrange("p (j f) -> p j f", j=TPG),
                                                rows[:, v, :, :], ALU.add).then_inc(s["message_summed"], 1)
                    if general and has(k, 4):
                        all_windows(0, k - 4)
                return step

            def norm_scale(n, c, u, busy=True, ts=BOTH):
                a, m, b = tiles_of(ts)
                dve.wait_ge(node[n]["std"], c + 1)
                nc.vector.reciprocal(rstd[:, u, a:b], std[:, u, a:b]).then_inc(node[n]["rstd"], 1)
                dve.wait_ge(node[n]["rstd"], c + 1)
                nc.vector.scalar_tensor_tensor(out=shift[:, u, a:b], in0=mv[:, u, a:b, 0], scalar=-1.0, in1=rstd[:, u, a:b],
                                               op0=ALU.mult, op1=ALU.mult).then_inc(node[n]["shift"], 1)
                if busy:
                    wait(dve, stored[n + 1][u], 16 * (c // 2))
                for j in range(a, m):
                    last = nc.vector.tensor_scalar(done_rows[:, u, j, :], nm[:, u, j, :], mv[:, u, j, 0:1], rstd[:, u, j:j + 1],
                                                   ALU.subtract, ALU.mult)
                last.then_inc(node[n]["rows_v"], 1)

            def row_stats(n, c, v, ts=BOTH):
                a, _, b = tiles_of(ts)
                wait_alone(dve, node[n]["added"], c + 1)
                for j in range(a, b):
                    last = nc.vector.bn_stats(stats[:, v, j, :], nm[:, v, j, :])
                last.then_inc(node[n]["stats"], 1)

            def moments(n, c, v, ts=BOTH):
                a, _, b = tiles_of(ts)
                wait_alone(dve, node[n]["stats"], c + 1)
                for j in range(a, b):
                    last = nc.vector.bn_aggr(mv[:, v, j, :], stats[:, v, j, :])
                last.then_inc(node[n]["mv"], 1)

            def messages_and_x(c, v, banks, ts=BOTH, counted=None):
                dve.wait_ge(node[0]["product"], (c if counted is None else counted) + 1)
                for t in ts:
                    a, b = SPAN[t]
                    last = nc.vector.scalar_tensor_tensor(out=nm[:, v, a:b, :], in0=x_rows[:, bass.ds(c * CT + a, b - a), :], scalar=2.0,
                                                          in1=as_rows(banks[t], t), op0=ALU.mult, op1=ALU.add)
                last.then_inc(node[0]["added"], 1)

            def means(n, c, u, ts=BOTH):
                a, _, b = tiles_of(ts)
                nodes_of = bass.ds(c * CN + a * P, (b - a) * P)
                nc.vector.tensor_tensor(fm[:, u, a * P:b * P], acc[n][:, nodes_of], degree[:, nodes_of],
                                        ALU.mult).then_inc(node[n]["lhs"], 1)

            def add_own(n, c, v, banks, ts=BOTH, counted=None):
                dve.wait_ge(node[n]["product"], (c if counted is None else counted) + 1)
                for t in ts:
                    a, b = SPAN[t]
                    last = nc.vector.tensor_tensor(nm[:, v, a:b, :], as_rows(banks[t], t),
                                                   own[:, bass.ds(c * CT + a, b - a), :], ALU.add)
                last.then_inc(node[n]["added"], 1)

            def inverse_degree(c):
                at = degree[:, bass.ds(c * CN, CN)]
                nc.vector.tensor_scalar(at, at, 1.0, None, ALU.max).then_inc(s["inverse"], 1)
                wait_alone(dve, s["inverse"], 2 * c + 1)
                nc.vector.reciprocal(at, at).then_inc(s["inverse"], 1)

            def nodes_any_order(n):
                def sums(c):
                    v = c % 2 if isinstance(c, int) else None
                    messages_and_x(c, v, pair(v))
                    row_stats(0, c, v)
                    moments(0, c, v)

                def free_means(c, u):
                    wait(dve, node[n]["product"], c - 1)
                    means(n, c, u)

                def free_add(c, v):
                    if n == 1:
                        wait(dve, node[1]["rows"], c - 1)
                    add_own(n, c, v, pair(v))
                    if n == 2:
                        row_stats(2, c, v)
                        moments(2, c, v)

                def nodes0(c, u, i):
                    norm_scale(0, c, u)
                    if is_chunk(c + 1):
                        sums(c + 1)

                def nodes1(c, u, i):
                    if is_chunk(c + 1):
                        free_means(c + 1, (u + 1) % 2)
                    free_add(c, u)

                def nodes2(c, u, i):
                    if is_chunk(c + 2):
                        free_means(c + 2, u)
                    norm_scale(2, c, u)
                    if is_chunk(c + 1):
                        free_add(c + 1, (u + 1) % 2)
                if n == 0:
                    sums(0)
                    over_chunks_unrolled(dve, nodes0)
                elif n == 1:
                    free_means(0, 0)
                    over_chunks(dve, nodes1)
                else:
                    free_means(0, 0)
                    free_means(1, 1)
                    free_add(0, 0)
                    over_chunks_unrolled(dve, nodes2)

            def hook_of(n):
                def hook(c, h):
                    if n > 0 and h == 0:
                        dve.wait_ge(s["window_added"], (c * BR + NODE_ROUND) * U - LAG + n * NG)
                        means(n, c, 0)
                    if h == 2:
                        (add_own(n, c, 0, pair(3)) if n > 0 else messages_and_x(c, 0, pair(3)))
                    if n != 1 and h == 3:
                        row_stats(n, c, 0)
                    if n != 1 and h == 4:
                        moments(n, c, 0)
                    if n != 1 and h == 5:
                        norm_scale(n, c, 0, False)
                    if n > 0 and h == 2 * U - 2 and isinstance(c, int):
                        dve.wait_ge(s["window_added"], LAST_DUE + n * NG)
                        means(n, NCH - 1, 1, (0,))
                    if n > 0 and h == 2 * U - 1 and isinstance(c, int):
                        last_sums(n, 0)
                return hook

            def last_sums(n, t):
                if n == 0:
                    messages_and_x(NCH - 1, 1, pair(3), (t,), NCH - 1 + t)
                else:
                    add_own(n, NCH - 1, 1, pair(3), (t,), NCH - 1 + t)
                if n != 1:
                    row_stats(n, NCH - 1 + t, 1, (t,))

            def last_chunk(n):
                if n > 0:
                    means(n, NCH - 1, 1, (1,))
                if n != 1:
                    moments(n, NCH - 1, 1, (0,))
                last_sums(n, 1)
                if n != 1:
                    norm_scale(n, NCH - 1, 1, False, (0,))
                    moments(n, NCH, 1, (1,))
                    norm_scale(n, NCH, 1, False, (1,))

            def all_phases(general):
                table_stored(dve, 0)
                if general:
                    over_steps(dve, step_of(True), 6)
                    dve.wait_ge(s["window_added"], NG)
                    nodes_any_order(0)
                else:
                    def last_steps(k):
                        if k == NG + 3:
                            last_sums(0, 0)
                    over_steps_and_chunks(dve, step_of(False), hook_of(0), until_stored(dve, 0), 6, last_steps)
                    last_chunk(0)
                nc.vector.memset(acc_b[:, :], 0.0).then_inc(s["acc_clear"], 1)
                dve.wait_ge(s["acc_clear"], 1)
                for ph in (1, 2):
                    def step(g, u, i, ph=ph):
                        if general:
                            all_windows(ph, g)
                            return
                        fast_one_hots(ph, g, u)
                        if not (isinstance(g, int) and g == 0):
                            fast_add(ph, g - 1, base_of(g - 1))
                    def groups(i, step=step):
                        for u in range(U):
                            step(i * U + u, u, i)
                    groups(0)
                    if ph == 1:
                        nc.vector.memset(acc_a[:, :], 0.0).then_inc(s["acc_clear"], 1)
                    with dve.Fori(0, NCH) as c:
                        groups(2 * c + 1)
                        groups(2 * c + 2)
                        if ph == 1:
                            inverse_degree(c)
                        project(ph, c, 0, None)
                    with dve.Fori(2 * NCH + 1, NG // U if general else NODE_ROUND) as i:
                        groups(i)
                    dve.wait_ge(proj[ph]["rows"], NCH)
                    if general:
                        dve.wait_ge(s["window_added"], (ph + 1) * NG)
                        table_stored(dve, ph)
                        nodes_any_order(ph)
                    else:
                        node_blocks(dve, step, NODE_ROUND, hook_of(ph), until_stored(dve, ph) if ph == 2 else lambda c: None)
                        fast_add(ph, NG - 1, base_of(NG - 1))
                        dve.wait_ge(s["window_added"], (ph + 1) * NG)
                        last_chunk(ph)

            spread = dve.value_load(flag[0:1, 0:1], min_val=0, max_val=1)
            with dve.If(spread == 0):
                all_phases(False)
            with dve.Else():
                all_phases(True)


_INS = ['x', 'src', 'dst', 'edge_attr_64', 'edge_weight', 'L0_gnn_We1', 'L0_gnn_be1', 'L0_gnn_We2', 'L0_gnn_be2',
        'L0_gnn_Wt', 'L0_gnn_bt', 'L0_gnn_Wn1', 'L0_gnn_bn1', 'L0_gnn_Wn2', 'L0_gnn_bn2', 'L1_gnn_W_rel0',
        'L1_gnn_b_rel0', 'L1_gnn_W_root0', 'L1_gnn_W_rel1', 'L1_gnn_b_rel1', 'L1_gnn_W_root1']
_OUT = ((6250, 128), 'float32')


def kernel(**inputs):
    import numpy as _np
    import concourse.bacc as _bacc
    from concourse import mybir as _mybir
    from concourse.bass_utils import run_bass_kernel_spmd as _run

    nc = _bacc.Bacc("TRN2", target_bir_lowering=False, num_devices=1)
    arrays, args = {}, []
    for name in _INS:
        a = _np.ascontiguousarray(inputs[name])
        arrays[f"in_{name}"] = a
        args.append(nc.dram_tensor(f"in_{name}", a.shape, _mybir.dt.from_np(a.dtype), kind="ExternalInput").ap())
    shape, dtype = _OUT
    args.append(nc.dram_tensor("out_0", shape, _mybir.dt.from_np(_np.dtype(dtype)), kind="ExternalOutput").ap())
    gnn_program(nc, *args)
    r = _run(nc, [arrays], core_ids=[0])
    return r.results[0]["out_0"]
```
